# Optimizing a Trainium2 kernel written in Bass

```python
import numpy as np
import jax
import jax.numpy as jnp

def _softmax(x, axis=-1):
    return jax.nn.softmax(x, axis=axis)

def _gelu(x):
    return jax.nn.gelu(x, approximate=True)

def _silu(x):
    return jax.nn.silu(x)

def _sigmoid(x):
    return jax.nn.sigmoid(x)

def _layernorm(x, axis=-1, eps=1e-05):
    m = jnp.mean(x, axis=axis, keepdims=True)
    v = jnp.var(x, axis=axis, keepdims=True)
    return (x - m) / jnp.sqrt(v + eps)

def _scatter_add(tgt, idx, src, axis=0):
    return tgt.at[idx].add(src)

def _segment_sum(src, seg, n):
    return jax.ops.segment_sum(src, seg, n)
kernel_name = 'mk_adaln_ffn_d1_seqx_r4_8b305b'

def setup_inputs(seed: int=0):
    np.random.seed(seed)
    _w = jnp.asarray

    def _rec_inputs():
        import jax
        import jax.numpy as jnp
        _rk = jax.random.key(seed)
        x = -0.000125 + 0.9999 * jax.random.normal(jax.random.fold_in(_rk, 1), (128, 64, 1024), jnp.float32)
        _lenS = 64 - jax.random.randint(jax.random.fold_in(_rk, 7), (128,), 0, max(1, 64 // 4) + 1, jnp.int32)
        _lenS2 = 64 - jax.random.randint(jax.random.fold_in(_rk, 8), (128,), 0, max(1, 64 // 4) + 1, jnp.int32)
        cond_128 = 0.0061147 + 1.02565 * jax.random.normal(jax.random.fold_in(_rk, 11), (128, 128), jnp.float32)
        return (x, cond_128)
    x, cond_128 = _rec_inputs()

    def _L0_cond_setup():
        import jax, jax.numpy as jnp
        import numpy as np
        K = 8
        T = 1.0
        D_EMBD = 128
        IN_C = 64
        OUT_C = 64
        BS = 32
        H = 1024
        HID = 128
        key = jax.random.key(seed)
        ks = jax.random.split(key, 10)
        s = lambda fan_in: 1.0 / np.sqrt(fan_in)
        return {'x': jax.random.normal(ks[0], (BS, IN_C, H), dtype=jnp.float32), 'embedding': jax.random.normal(ks[1], (BS, D_EMBD), dtype=jnp.float32), 'W0': jax.random.normal(ks[2], (D_EMBD, HID), dtype=jnp.float32) * s(D_EMBD), 'b0': jnp.zeros((HID,), dtype=jnp.float32), 'W1': jax.random.normal(ks[3], (HID, HID), dtype=jnp.float32) * s(HID), 'b1': jnp.zeros((HID,), dtype=jnp.float32), 'W2': jax.random.normal(ks[4], (HID, K), dtype=jnp.float32) * s(HID), 'b2': jnp.zeros((K,), dtype=jnp.float32), 'weight': jax.random.normal(ks[5], (K, OUT_C, IN_C, 1), dtype=jnp.float32) * s(IN_C), 'bias_k': jax.random.normal(ks[6], (K, OUT_C), dtype=jnp.float32) * 0.1}
    _L0_cond_all = _L0_cond_setup()
    _L0_cond_in = {k: v for k, v in _L0_cond_all.items() if k in ('W0', 'b0', 'W1', 'b1', 'W2', 'b2', 'weight', 'bias_k')}
    del _L0_cond_all

    def _L0_ffn_setup():
        import jax, jax.numpy as jnp
        import numpy as np
        R = 16
        ALPHA = 32
        SCALING = ALPHA / R
        E = 8
        TOP_K = 2
        key = jax.random.key(seed)
        ks = jax.random.split(key, 5)
        B, S, D = (4, 512, 1024)
        x = jax.random.normal(ks[0], (B, S, D), dtype=jnp.float32)
        base_W = jax.random.normal(ks[1], (D, D), dtype=jnp.float32) * 0.02
        router_W = jax.random.normal(ks[2], (E, D), dtype=jnp.float32) * 0.02
        lora_A = jax.random.normal(ks[3], (E, D, R), dtype=jnp.float32) * 0.02
        lora_B = jax.random.normal(ks[4], (E, R, D), dtype=jnp.float32) * 0.02
        return {'x': x, 'base_W': base_W, 'router_W': router_W, 'lora_A': lora_A, 'lora_B': lora_B}
    _L0_ffn_all = _L0_ffn_setup()
    _L0_ffn_in = {k: v for k, v in _L0_ffn_all.items() if k in ('base_W', 'router_W', 'lora_A', 'lora_B')}
    del _L0_ffn_all
    return {'x': x, 'cond_128': cond_128, 'L0_cond_W0': _L0_cond_in['W0'], 'L0_cond_b0': _L0_cond_in['b0'], 'L0_cond_W1': _L0_cond_in['W1'], 'L0_cond_b1': _L0_cond_in['b1'], 'L0_cond_W2': _L0_cond_in['W2'], 'L0_cond_b2': _L0_cond_in['b2'], 'L0_cond_weight': _L0_cond_in['weight'], 'L0_cond_bias_k': _L0_cond_in['bias_k'], 'L0_ffn_base_W': _L0_ffn_in['base_W'], 'L0_ffn_router_W': _L0_ffn_in['router_W'], 'L0_ffn_lora_A': _L0_ffn_in['lora_A'], 'L0_ffn_lora_B': _L0_ffn_in['lora_B']}

def reference(x, cond_128, L0_cond_W0, L0_cond_b0, L0_cond_W1, L0_cond_b1, L0_cond_W2, L0_cond_b2, L0_cond_weight, L0_cond_bias_k, L0_ffn_base_W, L0_ffn_router_W, L0_ffn_lora_A, L0_ffn_lora_B):
    import jax
    import jax.numpy as jnp

    def _L0_cond_ref(x, embedding, W0, b0, W1, b1, W2, b2, weight, bias_k):
        import jax, jax.numpy as jnp
        import numpy as np
        K = 8
        T = 1.0
        D_EMBD = 128
        IN_C = 64
        OUT_C = 64
        BS = 32
        H = 1024
        HID = 128
        h = jax.nn.gelu(embedding @ W0 + b0, approximate=False)
        h = jax.nn.gelu(h @ W1 + b1, approximate=False)
        att = jax.nn.softmax((h @ W2 + b2) / T, axis=-1)
        agg_w = jnp.einsum('bk,koi->boi', att, weight[..., 0])
        agg_b = att @ bias_k
        out = jnp.einsum('boi,bih->boh', agg_w, x) + agg_b[:, :, None]
        return out

    def _L0_ffn_ref(x, base_W, router_W, lora_A, lora_B):
        import jax, jax.numpy as jnp
        import numpy as np
        R = 16
        ALPHA = 32
        SCALING = ALPHA / R
        E = 8
        TOP_K = 2
        base = jnp.einsum('bsd,od->bso', x, base_W)
        logits = jnp.einsum('bsd,ed->bse', x, router_W)
        probs = jax.nn.softmax(logits.astype(jnp.float32), axis=-1)
        top_vals, top_idx = jax.lax.top_k(probs, TOP_K)
        rw = top_vals / jnp.sum(top_vals, axis=-1, keepdims=True)
        w_dense = jnp.sum(jax.nn.one_hot(top_idx, E, dtype=rw.dtype) * rw[..., None], axis=-2).astype(x.dtype)
        mid = jnp.einsum('bsd,edr->bser', x, lora_A)
        mid = mid * w_dense[..., None]
        inc = jnp.einsum('bser,erd->bsd', mid, lora_B)
        return base + inc * SCALING
    x = x + _L0_ffn_ref(_L0_cond_ref(x, cond_128, L0_cond_W0, L0_cond_b0, L0_cond_W1, L0_cond_b1, L0_cond_W2, L0_cond_b2, L0_cond_weight, L0_cond_bias_k), L0_ffn_base_W, L0_ffn_router_W, L0_ffn_lora_A, L0_ffn_lora_B)
    return x

_drawn_inputs = setup_inputs


def setup_inputs(seed=0):
    import zlib

    import numpy as np

    out = dict(_drawn_inputs(seed))
    spreads = {'L0_cond_b0': (0.0, 0.789), 'L0_cond_b1': (0.0, 0.468), 'L0_cond_b2': (0.0, 0.448)}
    factors = {}
    for name, (base, spread) in spreads.items():
        noise = np.random.default_rng([zlib.crc32(name.encode()), seed]).standard_normal(out[name].shape)
        drawn = base * np.exp(spread * noise) if base else spread * noise
        out[name] = jnp.asarray(drawn.astype(out[name].dtype))
    for name, factor in factors.items():
        out[name] = (out[name] * factor).astype(out[name].dtype)
    return out
```

```python
import concourse.bass as bass
from concourse import mybir
from contextlib import ExitStack


def adaln_ffn_kernel(nc, x, cond, w0, b0, w1, b1, w2, b2, weight, bias_k, base_w, router_w, lora_a, lora_b, out):
    f32, f32r = mybir.dt.float32, mybir.dt.float32r
    ALU, ACT, AX = mybir.AluOpType, mybir.ActivationFunctionType, mybir.AxisListType

    B, C, D = x.shape
    P = 128
    PAR = P // C
    NT = B // PAR
    NC = D // P
    K = weight.shape[0]
    E, _, R = lora_a.shape
    ER = E * R
    NW = D + ER + E
    LW = ER + E
    SCALING = 32 / 16
    BANK = 512
    HALF = NC // 2
    XR = 4
    WS = 4
    TOP = 2
    OG = BANK // NT

    x_t = x.rearrange("(t b) c d -> t (b c) d", b=PAR)
    out_t = out.rearrange("(t b) c d -> t (b c) d", b=PAR)
    bias_dram = nc.dram_tensor("bias_rows", [NT, PAR * C], f32)

    ctx = ExitStack()
    with ctx:
        def sb(name, shape, dt=f32):
            return ctx.enter_context(nc.sbuf_tensor(name, shape, dt))

        def sem(name):
            return ctx.enter_context(nc.semaphore(name))

        w_hi = sb("w_hi", [P, NC, NW], f32r)
        w_lo = sb("w_lo", [P, NC, NW], f32r)
        lb_hi = sb("lb_hi", [ER, D], f32r)
        lb_lo = sb("lb_lo", [ER, D], f32r)
        agg = sb("agg", [P, NT, C])
        x_sb = sb("x_sb", [P, XR, D])
        bias_sb = sb("bias_sb", [P, XR, P])
        x_hi = sb("x_hi", [P, 2, D], f32r)
        x_lo = sb("x_lo", [P, 2, D], f32r)
        a_raw = sb("a_raw", [P, XR, P])
        a_hi = sb("a_hi", [P, 2, P], f32r)
        a_lo = sb("a_lo", [P, 2, P], f32r)
        y_sum = sb("y_sum", [P, 2, BANK])
        y_hi = sb("y_hi", [P, 2, D], f32r)
        y_lo = sb("y_lo", [P, 2, D], f32r)
        out_sb = sb("out_sb", [P, 2, D])
        logits = sb("logits", [P, E])
        neg_max = sb("neg_max", [P, 1])
        beats = sb("beats", [P, E, 2 * E])
        ties = sb("ties", [P, E, E])
        earlier = sb("earlier", [P, E, E])
        rank = sb("rank", [P, E])
        chosen = sb("chosen", [P, E])
        exps = sb("exps", [P, E])
        picked = sb("picked", [P, E])
        total = sb("total", [P, 1])
        inv_total = sb("inv_total", [P, 1])
        gate = sb("gate", [P, E])
        mid = sb("mid", [P, ER])
        mid_hi = sb("mid_hi", [ER, P], f32r)
        mid_lo = sb("mid_lo", [ER, P], f32r)
        w_stage = sb("w_stage", [P, WS, D])
        la_raw = sb("la_raw", [P, NC, E, R])
        lb_raw = out_sb[:, 0, :]
        rw_raw = out_sb[0:E, 1, :]
        mixk = sb("mixk", [K, C, C])
        ident = sb("ident", [P, P])
        cond_sb = sb("cond_sb", [P, P])
        cond_t = sb("cond_t", [P, P])
        w0_sb, w1_sb = sb("w0_sb", [P, P]), sb("w1_sb", [P, P])
        w2_sb = sb("w2_sb", [P, K])
        b0_sb, b1_sb = sb("b0_sb", [P, 1]), sb("b1_sb", [P, 1])
        b2_sb = sb("b2_sb", [P, K])
        h1, h2 = sb("h1", [P, P]), sb("h2", [P, P])
        att = sb("att", [P, K])
        att_nm = sb("att_nm", [P, 1])
        att_sum = sb("att_sum", [P, 1])
        att_t = sb("att_t", [K, B])
        bk_sb = sb("bk_sb", [K, C])
        bias_rows = sb("bias_rows_sb", [B, C])

        acc = [[ctx.enter_context(nc.psum_tensor(f"acc{s}{h}", [P, BANK], f32)) for h in range(2)] for s in range(2)]
        side = [ctx.enter_context(nc.psum_tensor(f"side{s}", [P, BANK], f32)) for s in range(2)]
        y_ps = [ctx.enter_context(nc.psum_tensor(f"y_ps{h}", [P, BANK], f32)) for h in range(2)]
        MT = 256

        cond_in, mlp_in, mix_in, rw_in, la_in, lb_in = (sem(n) for n in (
            "cond_in", "mlp_in", "mix_in", "rw_in", "la_in", "lb_in"))
        w_in = [sem(f"w_in{s}") for s in range(WS)]
        zeros_set, consts_set = sem("zeros_set"), sem("consts_set")
        cond_on_pe, cond_t_ready = sem("cond_on_pe"), sem("cond_t_ready")
        mlp_mm, mlp_act, att_step, att_exp = sem("mlp_mm"), sem("mlp_act"), sem("att_step"), sem("att_exp")
        att_tr, att_t_ready, bias_mm, bias_ready, bias_out = (sem(n) for n in (
            "att_tr", "att_t_ready", "bias_mm", "bias_ready", "bias_out"))
        w_tr, w_hi_set, w_lo_set = sem("w_tr"), sem("w_hi_set"), sem("w_lo_set")
        rw_tr, rw_hi_set, rw_lo_set = sem("rw_tr"), sem("rw_hi_set"), sem("rw_lo_set")
        la_hi_set, la_lo_set, lb_hi_set, lb_lo_set = (sem(n) for n in (
            "la_hi_set", "la_lo_set", "lb_hi_set", "lb_lo_set"))
        agg_mm, agg_even, agg_odd = sem("agg_mm"), sem("agg_even"), sem("agg_odd")
        x_in = [sem(f"x_in{s}") for s in range(XR)]
        mix_w_in = [sem(f"mix_w_in{s}") for s in range(XR)]
        MIX_W = 16 * (PAR + 1)
        x_hi_ready, x_lo_ready, a_hi_ready, a_lo_ready = (sem(n) for n in (
            "x_hi_ready", "x_lo_ready", "a_hi_ready", "a_lo_ready"))
        mixed, y_sum_ready, y_hi_ready, y_lo_ready = (sem(n) for n in (
            "mixed", "y_sum_ready", "y_hi_ready", "y_lo_ready"))
        main_done, route_step, exps_ready, mid_tr, mid_hi_ready, mid_lo_ready = (sem(n) for n in (
            "main_done", "route_step", "exps_ready", "mid_tr", "mid_hi_ready", "mid_lo_ready"))
        up_done, out_ready = sem("up_done"), sem("out_ready")
        out_stored = [sem(f"out_stored{s}") for s in range(2)]

        ROUTE = 12

        def from_tile(t, n):
            return t >= n if isinstance(t, int) else True

        def before_tile(t, n):
            return t < n if isinstance(t, int) else True

        def over_tiles(eng, body):
            for t in range(XR):
                body(t, t)
            with eng.Fori(1, NT // XR - 1) as i:
                for k in range(XR):
                    body(i * XR + k, k)
            for t in range(NT - XR, NT):
                body(t, t % XR)

        block = ctx.enter_context(nc.Block())

        @block.sync
        def _(sp):
            sp.dma_start(cond_sb[:, :], cond).then_inc(cond_in, 16)
            sp.dma_start(w0_sb[:, :], w0).then_inc(mlp_in, 16)
            sp.dma_start(w1_sb[:, :], w1).then_inc(mlp_in, 16)
            sp.dma_start(w2_sb[:, :], w2).then_inc(mlp_in, 16)
            sp.dma_start(b0_sb[:, :], b0.rearrange("(p a) -> p a", a=1)).then_inc(mlp_in, 16)
            sp.dma_start(b1_sb[:, :], b1.rearrange("(p a) -> p a", a=1)).then_inc(mlp_in, 16)
            sp.dma_start(b2_sb[:, :], b2.partition_broadcast(P)).then_inc(mlp_in, 16)
            sp.dma_start(mixk[:, :, :], weight.rearrange("k o i a -> k o (i a)")).then_inc(mix_in, 16)
            sp.dma_start(bk_sb[:, :], bias_k).then_inc(mix_in, 16)
            for g in range(D // P):
                if g >= WS:
                    sp.wait_ge(w_tr, 2 * (g - WS + 1))
                sp.dma_start(w_stage[:, g % WS, :], base_w[g * P:(g + 1) * P, :]).then_inc(w_in[g % WS], 16)

            def mixing_weights(t, k):
                for b in range(PAR):
                    part = slice(b * C, (b + 1) * C)
                    sp.dma_start(a_raw[part, k, part], agg[part, t, :]).then_inc(mix_w_in[k], 16)
                sp.dma_start(bias_sb[:, k, :], bias_dram[t, :].partition_broadcast(P)).then_inc(mix_w_in[k], 16)

            def load(t, k):
                sp.wait_ge(out_ready, 2 * (t - XR) + 2)
                sp.dma_start(x_sb[:, k, :], x_t[t, :, :]).then_inc(x_in[k], 16)
                mixing_weights(t, k)

            for k in range(XR):
                sp.dma_start(x_sb[:, k, :], x_t[k, :, :]).then_inc(x_in[k], 16)
            sp.wait_ge(bias_ready, 1)
            sp.dma_start(bias_dram.rearrange("t (b c) -> (t b) c", b=PAR), bias_rows[:, :]).then_inc(bias_out, 16)
            sp.wait_ge(bias_out, 16)
            sp.wait_ge(agg_even, C // OG)
            sp.wait_ge(agg_odd, C // OG)
            sp.wait_ge(zeros_set, 3)
            for k in range(XR):
                mixing_weights(k, k)
            with sp.Fori(1, NT // XR) as i:
                for k in range(XR):
                    load(i * XR + k, k)

        @block.gpsimd
        def _(pool):
            nc.gpsimd.memset(ident[:, :], 0.0).then_inc(zeros_set, 1)
            nc.gpsimd.memset(earlier[:, :, :], 1.0).then_inc(zeros_set, 1)
            nc.gpsimd.memset(a_raw[:, :, :], 0.0).then_inc(zeros_set, 1)
            pool.wait_ge(zeros_set, 3)
            nc.gpsimd.affine_select(out=ident[:, :], in_=ident[:, :], compare_op=ALU.not_equal, fill=1.0,
                                    base=0, pattern=[[-1, P]], channel_multiplier=1).then_inc(consts_set, 1)
            nc.gpsimd.affine_select(out=earlier[:, :, :], in_=earlier[:, :, :], compare_op=ALU.is_gt, fill=0.0,
                                    base=0, pattern=[[1, E], [-1, E]], channel_multiplier=0).then_inc(consts_set, 1)
            pool.wait_ge(la_in, 16 * NC)
            la_v = la_raw[:, :, :, :].rearrange("p c e r -> p c (e r)")
            nc.gpsimd.tensor_copy(w_hi[:, :, D:D + ER], la_v).then_inc(la_hi_set, 1)
            pool.wait_ge(la_hi_set, 1)
            nc.gpsimd.tensor_tensor(w_lo[:, :, D:D + ER], la_v, w_hi[:, :, D:D + ER].bitcast(f32),
                                    ALU.subtract).then_inc(la_lo_set, 1)
            pool.wait_ge(lb_in, 16)
            nc.gpsimd.tensor_copy(lb_hi[:, :], lb_raw[:, :]).then_inc(lb_hi_set, 1)
            pool.wait_ge(lb_hi_set, 1)
            nc.gpsimd.tensor_tensor(lb_lo[:, :], lb_raw[:, :], lb_hi[:, :].bitcast(f32),
                                    ALU.subtract).then_inc(lb_lo_set, 1)

        @block.tensor
        def _(pe):
            def transpose_w(g):
                pe.wait_ge(w_in[g % WS], 16 * (g // WS + 1))
                for h in range(2):
                    if g >= 2:
                        pe.wait_ge(w_lo_set, 2 * (g - 2) + h + 1)
                    for j in range(HALF):
                        c = h * HALF + j
                        last = nc.tensor.transpose(acc[g % 2][h][:, j * P:(j + 1) * P],
                                                   w_stage[:, g % WS, c * P:(c + 1) * P], ident[:, :])
                    last.then_inc(w_tr, 1)

            att_tb = att_t[:, :].rearrange("k (t b) -> k t b", b=PAR)

            def mixing_kernels(n):
                if n >= 2:
                    pe.wait_ge(agg_even, n - 1)
                    pe.wait_ge(agg_odd, n - 1)
                for j in range(OG):
                    for b in range(PAR):
                        last = nc.tensor.matmul(y_ps[n % 2][b * C:(b + 1) * C, j * NT:(j + 1) * NT],
                                                mixk[:, OG * n + j, :], att_tb[:, :, b], start=True, stop=True)
                last.then_inc(agg_mm, 1)

            pe.wait_ge(consts_set, 2)
            pe.wait_ge(cond_in, 16)
            nc.tensor.transpose(side[0][:, 0:P], cond_sb[:, :], ident[:, :]).then_inc(cond_on_pe, 1)
            transpose_w(0)
            pe.wait_ge(cond_t_ready, 1)
            pe.wait_ge(mlp_in, 16 * 6)
            nc.tensor.matmul(side[1][:, 0:P], w0_sb[:, :], cond_t[:, :], start=True, stop=True).then_inc(mlp_mm, 1)
            transpose_w(1)
            pe.wait_ge(mlp_act, 1)
            nc.tensor.matmul(side[0][:, 0:P], w1_sb[:, :], h1[:, :], start=True, stop=True).then_inc(mlp_mm, 1)
            transpose_w(2)
            pe.wait_ge(mlp_act, 2)
            nc.tensor.matmul(side[1][:, 0:K], h2[:, :], w2_sb[:, :], start=True, stop=True).then_inc(mlp_mm, 1)
            transpose_w(3)
            pe.wait_ge(att_step, 4)
            nc.tensor.transpose(side[0][0:K, 0:B], att[:, :], ident[:, :]).then_inc(att_tr, 1)
            pe.wait_ge(rw_in, 16)
            for c in range(NC):
                last = nc.tensor.transpose(side[1][:, c * E:(c + 1) * E], rw_raw[:, c * P:(c + 1) * P],
                                           ident[0:E, 0:E])
            last.then_inc(rw_tr, 1)
            pe.wait_ge(mix_in, 32)
            pe.wait_ge(att_t_ready, 1)
            nc.tensor.matmul(side[0][:, 0:C], att_t[:, :], bk_sb[:, :], start=True, stop=True).then_inc(bias_mm, 1)
            for n in range(C // OG):
                mixing_kernels(n)
                if n % 2 == 1:
                    transpose_w(4 + n // 2)

            def mix_chunk(t, k, c):
                s, h, j = k % 2, c // HALF, c % HALF
                if c == 0:
                    pe.wait_ge(x_hi_ready, t + 1)
                    pe.wait_ge(x_lo_ready, t + 1)
                    pe.wait_ge(a_hi_ready, t + 1)
                    pe.wait_ge(a_lo_ready, t + 1)
                if j == 0:
                    if isinstance(t, int) and t == 0:
                        pe.wait_ge(agg_even, C // OG)
                        pe.wait_ge(agg_odd, C // OG)
                    else:
                        pe.wait_ge(y_sum_ready, 2 * (t - 1) + h + 1)
                cols = slice(c * P, (c + 1) * P)
                o = y_ps[h][:, j * P:(j + 1) * P]
                nc.tensor.matmul(o, x_hi[:, s, cols], a_hi[:, s, :], start=True, stop=False)
                nc.tensor.matmul(o, x_hi[:, s, cols], a_lo[:, s, :], start=False, stop=False)
                last = nc.tensor.matmul(o, x_lo[:, s, cols], a_hi[:, s, :], start=False, stop=True)
                if j == HALF - 1:
                    last.then_inc(mixed, 1)

            def main_chunk(t, k, c):
                s = k % 2
                if c % HALF == 0:
                    pe.wait_ge(y_hi_ready, 2 * t + c // HALF + 1)
                    pe.wait_ge(y_lo_ready, 2 * t + c // HALF + 1)
                if c == 0 and from_tile(t, 2):
                    pe.wait_ge(out_ready, 2 * (t - 2) + 2)
                cols = slice(c * P, (c + 1) * P)
                groups = ((acc[s][0][:, :], slice(0, BANK), False), (acc[s][1][:, :], slice(BANK, 2 * BANK), False),
                          (side[s][:, 0:LW], slice(D, NW), True))
                for y, w, first, final in ((y_hi, w_hi, True, False), (y_hi, w_lo, False, False),
                                           (y_lo, w_hi, False, True)):
                    for o, wc, closes in groups:
                        last = nc.tensor.matmul(o, y[:, s, cols], w[:, c, wc], start=(c == 0 and first),
                                                stop=(closes and c == NC - 1 and final))
                if c == NC - 1:
                    last.then_inc(main_done, 1)

            def transpose_mid(t, k):
                pe.wait_ge(route_step, ROUTE * t + ROUTE)
                nc.tensor.transpose(side[k % 2][:, MT:MT + P], mid[:, :], ident[:, :]).then_inc(mid_tr, 1)

            def up(t, k):
                s = k % 2
                pe.wait_ge(mid_hi_ready, t + 1)
                pe.wait_ge(mid_lo_ready, t + 1)
                for m, w, final in ((mid_hi, lb_hi, False), (mid_hi, lb_lo, False), (mid_lo, lb_hi, True)):
                    for h in range(2):
                        last = nc.tensor.matmul(acc[s][h][:, :], m[:, :], w[:, h * BANK:(h + 1) * BANK],
                                                start=False, stop=final)
                last.then_inc(up_done, 1)

            for c in range(NC):
                mix_chunk(0, 0, c)
            pe.wait_ge(w_hi_set, 2 * NC)
            pe.wait_ge(w_lo_set, 2 * NC)
            pe.wait_ge(rw_hi_set, 1)
            pe.wait_ge(rw_lo_set, 1)
            pe.wait_ge(la_lo_set, 1)
            pe.wait_ge(lb_lo_set, 1)

            def tile(t, k):
                for c in range(NC):
                    main_chunk(t, k, c)
                    if before_tile(t, NT - 1):
                        mix_chunk(t + 1, (k + 1) % XR, c)
                    if c == 2 and from_tile(t, 1):
                        transpose_mid(t - 1, (k - 1) % XR)
                    if c == 4 and from_tile(t, 1):
                        up(t - 1, (k - 1) % XR)

            over_tiles(pe, tile)
            transpose_mid(NT - 1, (NT - 1) % XR)
            up(NT - 1, (NT - 1) % XR)

        @block.scalar
        def _(act):
            act.dma_start(rw_raw[:, :], router_w).then_inc(rw_in, 16)
            for c in range(NC):
                act.dma_start(la_raw[:, c, :, :],
                              lora_a[:, c * P:(c + 1) * P, :].rearrange("e p r -> p e r")).then_inc(la_in, 16)
            act.dma_start(lb_raw[:, :], lora_b.rearrange("e r d -> (e r) d")).then_inc(lb_in, 16)

            def take_w(g):
                for h in range(2):
                    act.wait_ge(w_tr, 2 * g + h + 1)
                    nc.scalar.activation(w_hi[:, h * HALF:(h + 1) * HALF, g * P:(g + 1) * P],
                                         acc[g % 2][h][:, :].rearrange("p (c n) -> p c n", c=HALF),
                                         ACT.Copy).then_inc(w_hi_set, 1)

            take_w(0)
            act.wait_ge(mlp_mm, 1)
            nc.scalar.activation(h1[:, :], side[1][:, 0:P], ACT.Gelu, bias=b0_sb[:, :]).then_inc(mlp_act, 1)
            take_w(1)
            act.wait_ge(mlp_mm, 2)
            nc.scalar.activation(h2[:, :], side[0][:, 0:P], ACT.Gelu, bias=b1_sb[:, :]).then_inc(mlp_act, 1)
            take_w(2)
            act.wait_ge(att_step, 2)
            nc.scalar.activation(exps[:, :], att[:, :], ACT.Exp, bias=att_nm[:, :],
                                 accum_out=att_sum[:, :]).then_inc(att_exp, 1)
            take_w(3)
            for n in range(C // OG):
                act.wait_ge(agg_mm, n + 1)
                nc.scalar.activation(agg[0:C, :, OG * n:OG * n + OG],
                                     y_ps[n % 2][0:C, :].rearrange("p (o t) -> p t o", o=OG),
                                     ACT.Copy).then_inc(agg_even, 1)
                if n % 2 == 1:
                    take_w(4 + n // 2)
            act.wait_ge(rw_tr, 1)
            nc.scalar.activation(w_hi[:, :, D + ER:NW], side[1][:, 0:NC * E].rearrange("p (c e) -> p c e", c=NC),
                                 ACT.Copy).then_inc(rw_hi_set, 1)

            def split_x(t, k):
                act.wait_ge(x_in[k], (t - k) * (16 // XR) + 16)
                if from_tile(t, 2):
                    act.wait_ge(mixed, 2 * (t - 2) + 2)
                nc.scalar.activation(x_hi[:, k % 2, :], x_sb[:, k, :], ACT.Copy).then_inc(x_hi_ready, 1)
                act.wait_ge(mix_w_in[k], (t - k) * (MIX_W // XR) + MIX_W)
                nc.scalar.activation(a_hi[:, k % 2, :], a_raw[:, k, :], ACT.Copy).then_inc(a_hi_ready, 1)

            def split_y(t, k, h):
                act.wait_ge(y_sum_ready, 2 * t + h + 1)
                if from_tile(t, 2):
                    act.wait_ge(main_done, t - 1)
                nc.scalar.activation(y_hi[:, k % 2, h * BANK:(h + 1) * BANK], y_sum[:, h, :],
                                     ACT.Copy).then_inc(y_hi_ready, 1)

            def exponents(t, k):
                act.wait_ge(route_step, ROUTE * t + 2)
                nc.scalar.activation(exps[:, :], logits[:, :], ACT.Exp, bias=neg_max[:, :]).then_inc(exps_ready, 1)

            def split_mid(t, k):
                act.wait_ge(mid_tr, t + 1)
                if from_tile(t, 1):
                    act.wait_ge(up_done, t)
                nc.scalar.activation(mid_hi[:, :], side[k % 2][:, MT:MT + P], ACT.Copy).then_inc(mid_hi_ready, 1)

            split_x(0, 0)
            split_x(1, 1)
            split_y(0, 0, 0)

            def tile(t, k):
                if from_tile(t, 1):
                    exponents(t - 1, (k - 1) % XR)
                split_y(t, k, 1)
                if before_tile(t, NT - 2):
                    split_x(t + 2, (k + 2) % XR)
                if from_tile(t, 1):
                    split_mid(t - 1, (k - 1) % XR)
                if before_tile(t, NT - 1):
                    split_y(t + 1, (k + 1) % XR, 0)
                if from_tile(t, 1):
                    store(t - 1, (k - 1) % XR)

            def store(t, k):
                act.wait_ge(out_ready, 2 * t + 2)
                act.dma_start(out_t[t, :, :], out_sb[:, k % 2, :]).then_inc(out_stored[k % 2], 16)

            over_tiles(act, tile)
            exponents(NT - 1, (NT - 1) % XR)
            split_mid(NT - 1, (NT - 1) % XR)
            store(NT - 1, (NT - 1) % XR)
            for s in range(2):
                act.wait_ge(out_stored[s], 16 * (NT // 2))

        @block.vector
        def _(dve):
            def take_w(g):
                for h in range(2):
                    dve.wait_ge(w_hi_set, 2 * g + h + 1)
                    w = (slice(None), slice(h * HALF, (h + 1) * HALF), slice(g * P, (g + 1) * P))
                    nc.vector.tensor_tensor(w_lo[w], acc[g % 2][h][:, :].rearrange("p (c n) -> p c n", c=HALF),
                                            w_hi[w].bitcast(f32), ALU.subtract).then_inc(w_lo_set, 1)

            dve.wait_ge(cond_on_pe, 1)
            nc.vector.tensor_copy(cond_t[:, :], side[0][:, 0:P]).then_inc(cond_t_ready, 1)
            take_w(0)
            take_w(1)
            take_w(2)
            dve.wait_ge(mlp_mm, 3)
            nc.vector.tensor_tensor(att[:, :], side[1][:, 0:K], b2_sb[:, :], ALU.add).then_inc(att_step, 1)
            dve.wait_ge(att_step, 1)
            nc.vector.tensor_reduce(att_nm[:, :], att[:, :], AX.X, ALU.max, negate=True).then_inc(att_step, 1)
            dve.wait_ge(att_exp, 1)
            nc.vector.reciprocal(att_sum[:, :], att_sum[:, :]).then_inc(att_step, 1)
            dve.wait_ge(att_step, 3)
            nc.vector.tensor_scalar(att[:, :], exps[:, :], att_sum[:, :], None, ALU.mult).then_inc(att_step, 1)
            dve.wait_ge(att_tr, 1)
            nc.vector.tensor_copy(att_t[:, :], side[0][0:K, 0:B]).then_inc(att_t_ready, 1)
            take_w(3)
            dve.wait_ge(bias_mm, 1)
            nc.vector.tensor_copy(bias_rows[:, :], side[0][:, 0:C]).then_inc(bias_ready, 1)
            for n in range(C // OG):
                dve.wait_ge(agg_mm, n + 1)
                nc.vector.tensor_copy(agg[C:P, :, OG * n:OG * n + OG],
                                      y_ps[n % 2][C:P, :].rearrange("p (o t) -> p t o", o=OG)).then_inc(agg_odd, 1)
                if n % 2 == 1:
                    take_w(4 + n // 2)
            dve.wait_ge(rw_hi_set, 1)
            rw = (slice(None), slice(None), slice(D + ER, NW))
            nc.vector.tensor_tensor(w_lo[rw], side[1][:, 0:NC * E].rearrange("p (c e) -> p c e", c=NC),
                                    w_hi[rw].bitcast(f32), ALU.subtract).then_inc(rw_lo_set, 1)

            def split_x(t, k):
                dve.wait_ge(x_hi_ready, t + 1)
                nc.vector.tensor_tensor(x_lo[:, k % 2, :], x_sb[:, k, :], x_hi[:, k % 2, :].bitcast(f32),
                                        ALU.subtract).then_inc(x_lo_ready, 1)
                dve.wait_ge(a_hi_ready, t + 1)
                nc.vector.tensor_tensor(a_lo[:, k % 2, :], a_raw[:, k, :], a_hi[:, k % 2, :].bitcast(f32),
                                        ALU.subtract).then_inc(a_lo_ready, 1)

            def add_bias(t, k, h):
                dve.wait_ge(mixed, 2 * t + h + 1)
                nc.vector.tensor_tensor(y_sum[:, h, :].rearrange("p (c r) -> p c r", c=HALF),
                                        y_ps[h][:, :].rearrange("p (c r) -> p c r", c=HALF),
                                        bias_sb[:, k, :].unsqueeze(1).broadcast_to([P, HALF, P]),
                                        ALU.add).then_inc(y_sum_ready, 1)

            def split_y(t, k, h):
                dve.wait_ge(y_hi_ready, 2 * t + h + 1)
                cols = slice(h * BANK, (h + 1) * BANK)
                nc.vector.tensor_tensor(y_lo[:, k % 2, cols], y_sum[:, h, :], y_hi[:, k % 2, cols].bitcast(f32),
                                        ALU.subtract).then_inc(y_lo_ready, 1)

            def route_logits(t, k):
                dve.wait_ge(main_done, t + 1)
                nc.vector.tensor_copy(logits[:, :], side[k % 2][:, ER:LW]).then_inc(route_step, 1)
                dve.wait_ge(route_step, ROUTE * t + 1)
                nc.vector.tensor_reduce(neg_max[:, :], logits[:, :], AX.X, ALU.max, negate=True).then_inc(route_step, 1)

            def route_choice(t, k):
                other = logits[:, :].unsqueeze(1).broadcast_to([P, E, E])
                own = logits[:, :].unsqueeze(2).broadcast_to([P, E, E])
                nc.vector.tensor_tensor(beats[:, :, 0:E], other, own, ALU.is_gt).then_inc(route_step, 1)
                nc.vector.tensor_tensor(ties[:, :, :], other, own, ALU.is_equal).then_inc(route_step, 1)
                dve.wait_ge(route_step, ROUTE * t + 4)
                nc.vector.tensor_tensor(beats[:, :, E:2 * E], ties[:, :, :], earlier[:, :, :],
                                        ALU.mult).then_inc(route_step, 1)
                dve.wait_ge(route_step, ROUTE * t + 5)
                nc.vector.tensor_reduce(rank[:, :], beats[:, :, :], AX.X, ALU.add).then_inc(route_step, 1)
                dve.wait_ge(route_step, ROUTE * t + 6)
                nc.vector.tensor_scalar(chosen[:, :], rank[:, :], float(TOP), None, ALU.is_lt).then_inc(route_step, 1)

            def route_weigh(t, k):
                dve.wait_ge(route_step, ROUTE * t + 7)
                dve.wait_ge(exps_ready, t + 1)
                nc.vector.tensor_tensor(picked[:, :], exps[:, :], chosen[:, :], ALU.mult).then_inc(route_step, 1)
                dve.wait_ge(route_step, ROUTE * t + 8)
                nc.vector.tensor_reduce(total[:, :], picked[:, :], AX.X, ALU.add).then_inc(route_step, 1)
                dve.wait_ge(route_step, ROUTE * t + 9)
                nc.vector.reciprocal(inv_total[:, :], total[:, :]).then_inc(route_step, 1)
                dve.wait_ge(route_step, ROUTE * t + 10)
                nc.vector.tensor_scalar(gate[:, :], picked[:, :], inv_total[:, :], SCALING,
                                        ALU.mult, ALU.mult).then_inc(route_step, 1)
                dve.wait_ge(route_step, ROUTE * t + 11)
                if from_tile(t, 1):
                    dve.wait_ge(mid_tr, t)
                nc.vector.tensor_tensor(mid[:, :].rearrange("p (e r) -> p e r", e=E),
                                        side[k % 2][:, 0:ER].rearrange("p (e r) -> p e r", e=E),
                                        gate[:, :].unsqueeze(2).broadcast_to([P, E, R]),
                                        ALU.mult).then_inc(route_step, 1)

            def split_mid(t, k):
                dve.wait_ge(mid_hi_ready, t + 1)
                nc.vector.tensor_tensor(mid_lo[:, :], side[k % 2][:, MT:MT + P], mid_hi[:, :].bitcast(f32),
                                        ALU.subtract).then_inc(mid_lo_ready, 1)

            def add_x(t, k):
                dve.wait_ge(up_done, t + 1)
                if from_tile(t, 2):
                    dve.wait_ge(out_stored[k % 2], 8 * (t - k % 2))
                for h in range(2):
                    cols = slice(h * BANK, (h + 1) * BANK)
                    nc.vector.tensor_tensor(out_sb[:, k % 2, cols], acc[k % 2][h][:, :], x_sb[:, k, cols],
                                            ALU.add).then_inc(out_ready, 1)

            split_x(0, 0)
            split_x(1, 1)
            add_bias(0, 0, 0)
            split_y(0, 0, 0)

            def tile(t, k):
                if from_tile(t, 1):
                    route_logits(t - 1, (k - 1) % XR)
                add_bias(t, k, 1)
                if from_tile(t, 1):
                    route_choice(t - 1, (k - 1) % XR)
                    route_weigh(t - 1, (k - 1) % XR)
                split_y(t, k, 1)
                if before_tile(t, NT - 2):
                    split_x(t + 2, (k + 2) % XR)
                if from_tile(t, 1):
                    split_mid(t - 1, (k - 1) % XR)
                if before_tile(t, NT - 1):
                    add_bias(t + 1, (k + 1) % XR, 0)
                    split_y(t + 1, (k + 1) % XR, 0)
                if from_tile(t, 1):
                    add_x(t - 1, (k - 1) % XR)

            over_tiles(dve, tile)
            last = (NT - 1, (NT - 1) % XR)
            route_logits(*last)
            route_choice(*last)
            route_weigh(*last)
            split_mid(*last)
            add_x(*last)

    return nc


_INS = ['x', 'cond_128', 'L0_cond_W0', 'L0_cond_b0', 'L0_cond_W1', 'L0_cond_b1', 'L0_cond_W2', 'L0_cond_b2',
        'L0_cond_weight', 'L0_cond_bias_k', 'L0_ffn_base_W', 'L0_ffn_router_W', 'L0_ffn_lora_A', 'L0_ffn_lora_B']


def kernel(**inputs):
    import numpy as np
    import concourse.bacc as bacc
    from concourse.bass_utils import run_bass_kernel_spmd

    nc = bacc.Bacc("TRN2", target_bir_lowering=False, num_devices=1)
    arrays, args = {}, []
    for name in _INS:
        a = np.ascontiguousarray(inputs[name])
        arrays[f"in_{name}"] = a
        args.append(nc.dram_tensor(f"in_{name}", a.shape, mybir.dt.from_np(a.dtype), kind="ExternalInput").ap())
    shape = inputs['x'].shape
    args.append(nc.dram_tensor("out", shape, mybir.dt.float32, kind="ExternalOutput").ap())
    adaln_ffn_kernel(nc, *args)
    r = run_bass_kernel_spmd(nc, [arrays], core_ids=[0])
    return r.results[0]["out"]
```

```python
import concourse.bass as bass
from concourse import mybir
from contextlib import ExitStack


def adaln_ffn_kernel(nc, x, cond, w0, b0, w1, b1, w2, b2, weight, bias_k, base_w, router_w, lora_a, lora_b, out):
    f32, f32r = mybir.dt.float32, mybir.dt.float32r
    ALU, ACT, AX = mybir.AluOpType, mybir.ActivationFunctionType, mybir.AxisListType

    B, C, D = x.shape
    P = 128
    PAR = P // C
    NT = B // PAR
    NC = D // P
    K = weight.shape[0]
    E, _, R = lora_a.shape
    ER = E * R
    NW = D + ER + E
    GW = -(-NW // 3 // 4) * 4
    GROUPS = [(0, GW), (GW, 2 * GW), (2 * GW, NW)]
    SIDE = D - 2 * GW
    SCALING = 32 / 16
    BANK = 512
    HALF = NC // 2
    XR = 4
    TOP = 2
    OG = BANK // B
    NA = C // PAR // OG

    x_t = x.rearrange("(t b) c d -> t (b c) d", b=PAR)
    out_t = out.rearrange("(t b) c d -> t (b c) d", b=PAR)
    bias_dram = nc.dram_tensor("bias_rows", [NT, PAR * C], f32)

    ctx = ExitStack()
    with ctx:
        def sb(name, shape, dt=f32):
            return ctx.enter_context(nc.sbuf_tensor(name, shape, dt))

        def sem(name):
            return ctx.enter_context(nc.semaphore(name))

        w_hi = sb("w_hi", [P, NC, NW], f32r)
        w_lo = sb("w_lo", [P, NC, NW], f32r)
        lb_hi = sb("lb_hi", [ER, D], f32r)
        lb_lo = sb("lb_lo", [ER, D], f32r)
        agg = sb("agg", [P, NT, C])
        x_sb = sb("x_sb", [P, XR, D])
        bias_sb = sb("bias_sb", [P, XR, P])
        mix_w = sb("mix_w", [P, XR, P])
        y_sum = sb("y_sum", [P, 2, BANK])
        y_hi = sb("y_hi", [P, 2, D], f32r)
        y_lo = sb("y_lo", [P, 2, D], f32r)
        out_sb = sb("out_sb", [P, 2, D])
        logits = sb("logits", [P, E])
        neg_max = sb("neg_max", [P, 1])
        beats = sb("beats", [P, E, 2 * E])
        ties = sb("ties", [P, E, E])
        earlier = sb("earlier", [P, E, E])
        rank = sb("rank", [P, E])
        chosen = sb("chosen", [P, E])
        exps = sb("exps", [P, E])
        picked = sb("picked", [P, E])
        total = sb("total", [P, 1])
        inv_total = sb("inv_total", [P, 1])
        gate = sb("gate", [P, E])
        mid = sb("mid", [P, ER])
        mid_hi = sb("mid_hi", [ER, P], f32r)
        mid_lo = sb("mid_lo", [ER, P], f32r)
        w_stage = sb("w_stage", [P, D // P, D])
        lmix_w = sb("lmix_w", [P, NC, E, R])
        lb_raw = out_sb[:, 0, :]
        rw_raw = out_sb[0:E, 1, :]
        mixk = sb("mixk", [K, C, C])
        ident = sb("ident", [P, P])
        cond_sb = sb("cond_sb", [P, P])
        cond_t = sb("cond_t", [P, P])
        w0_sb, w1_sb = sb("w0_sb", [P, P]), sb("w1_sb", [P, P])
        w2_sb = sb("w2_sb", [P, K])
        b0_sb, b1_sb = sb("b0_sb", [P, 1]), sb("b1_sb", [P, 1])
        b2_sb = sb("b2_sb", [P, K])
        h1, h2 = sb("h1", [P, P]), sb("h2", [P, P])
        att = sb("att", [P, K])
        att_nm = sb("att_nm", [P, 1])
        att_sum = sb("att_sum", [P, 1])
        att_t = sb("att_t", [K, B])
        bk_sb = sb("bk_sb", [K, C])
        bias_rows = sb("bias_rows_sb", [B, C])

        acc = [[ctx.enter_context(nc.psum_tensor(f"acc{s}{h}", [P, BANK], f32)) for h in range(3)] for s in range(2)]
        y_ps = [ctx.enter_context(nc.psum_tensor(f"y_ps{h}", [P, BANK], f32)) for h in range(2)]
        side = [acc[s][2] for s in range(2)]
        MID = slice(SIDE, SIDE + ER)
        mid_ps = y_ps[1][:, 0:P]

        cond_in, mlp_in, mix_in, rw_in, la_in, lb_in = (sem(n) for n in (
            "cond_in", "mlp_in", "mix_in", "rw_in", "la_in", "lb_in"))
        w_in = [sem(f"w_in{s}") for s in range(D // P)]
        zeros_set, consts_set = sem("zeros_set"), sem("consts_set")
        cond_on_pe, cond_t_ready = sem("cond_on_pe"), sem("cond_t_ready")
        mlp_mm, mlp_act, att_step, att_exp = sem("mlp_mm"), sem("mlp_act"), sem("att_step"), sem("att_exp")
        att_tr, att_t_ready, bias_mm, bias_ready, bias_out = (sem(n) for n in (
            "att_tr", "att_t_ready", "bias_mm", "bias_ready", "bias_out"))
        w_tr, w_hi_set, w_lo_set = sem("w_tr"), sem("w_hi_set"), sem("w_lo_set")
        rw_tr, rw_hi_set, rw_lo_set = sem("rw_tr"), sem("rw_hi_set"), sem("rw_lo_set")
        la_hi_set, la_lo_set, lb_hi_set, lb_lo_set = (sem(n) for n in (
            "la_hi_set", "la_lo_set", "lb_hi_set", "lb_lo_set"))
        agg_mm, agg_act, agg_dve = sem("agg_mm"), sem("agg_act"), sem("agg_dve")
        x_in = [sem(f"x_in{s}") for s in range(XR)]
        mix_w_in = [sem(f"mix_w_in{s}") for s in range(XR)]
        MIX_W = 16 * (PAR + 1)
        mixed, y_sum_ready, y_hi_ready, y_lo_ready = (sem(n) for n in (
            "mixed", "y_sum_ready", "y_hi_ready", "y_lo_ready"))
        main_done, route_step, exps_ready, mid_tr, mid_hi_ready, mid_lo_ready = (sem(n) for n in (
            "main_done", "route_step", "exps_ready", "mid_tr", "mid_hi_ready", "mid_lo_ready"))
        up_done, out_ready = sem("up_done"), sem("out_ready")
        out_stored = [sem(f"out_stored{s}") for s in range(2)]

        ROUTE = 12

        def from_tile(t, n):
            return t >= n if isinstance(t, int) else True

        def before_tile(t, n):
            return t < n if isinstance(t, int) else True

        def over_tiles(eng, body):
            for t in range(XR):
                body(t, t)
            with eng.Fori(1, NT // XR - 1) as i:
                for k in range(XR):
                    body(i * XR + k, k)
            for t in range(NT - XR, NT):
                body(t, t % XR)

        def take_agg(eng, copy, taken, n, o):
            eng.wait_ge(agg_mm, n + 1)
            for b in range(PAR):
                src = y_ps[n % 2][o * C:(o + 1) * C, :].rearrange("i (j t b) -> i b t j", j=OG, b=PAR)[:, b, :, :]
                dst = agg[b * C:(b + 1) * C, :, :].rearrange("i t (n j o) -> i n o t j", j=OG, o=PAR)[:, n, o, :, :]
                copy(dst, src).then_inc(taken, 1)

        block = ctx.enter_context(nc.Block())

        @block.sync
        def _(sp):
            sp.dma_start(cond_sb[:, :], cond).then_inc(cond_in, 16)
            sp.dma_start(w0_sb[:, :], w0).then_inc(mlp_in, 16)
            sp.dma_start(w1_sb[:, :], w1).then_inc(mlp_in, 16)
            sp.dma_start(w2_sb[:, :], w2).then_inc(mlp_in, 16)
            sp.dma_start(b0_sb[:, :], b0.rearrange("(p a) -> p a", a=1)).then_inc(mlp_in, 16)
            sp.dma_start(b1_sb[:, :], b1.rearrange("(p a) -> p a", a=1)).then_inc(mlp_in, 16)
            sp.dma_start(b2_sb[:, :], b2.partition_broadcast(P)).then_inc(mlp_in, 16)
            sp.dma_start(mixk[:, :, :], weight.rearrange("k o i a -> k o (i a)")).then_inc(mix_in, 16)
            sp.dma_start(bk_sb[:, :], bias_k).then_inc(mix_in, 16)
            for g in range(D // P):
                sp.dma_start(w_stage[:, g, :], base_w[g * P:(g + 1) * P, :]).then_inc(w_in[g], 16)

            def mixing_weights(t, k):
                for b in range(PAR):
                    part = slice(b * C, (b + 1) * C)
                    sp.dma_start(mix_w[part, k, part], agg[part, t, :]).then_inc(mix_w_in[k], 16)
                sp.dma_start(bias_sb[:, k, :], bias_dram[t, :].partition_broadcast(P)).then_inc(mix_w_in[k], 16)

            def load(t, k):
                sp.wait_ge(out_ready, 3 * (t - XR) + 3)
                sp.dma_start(x_sb[:, k, :], x_t[t, :, :]).then_inc(x_in[k], 16)
                mixing_weights(t, k)

            for k in range(XR):
                sp.dma_start(x_sb[:, k, :], x_t[k, :, :]).then_inc(x_in[k], 16)
            sp.wait_ge(bias_ready, 1)
            sp.dma_start(bias_dram.rearrange("t (b c) -> (t b) c", b=PAR), bias_rows[:, :]).then_inc(bias_out, 16)
            sp.wait_ge(bias_out, 16)
            sp.wait_ge(agg_act, PAR * NA)
            sp.wait_ge(agg_dve, PAR * NA)
            sp.wait_ge(zeros_set, 3)
            for k in range(XR):
                mixing_weights(k, k)
            with sp.Fori(1, NT // XR) as i:
                for k in range(XR):
                    load(i * XR + k, k)

        @block.gpsimd
        def _(pool):
            nc.gpsimd.memset(ident[:, :], 0.0).then_inc(zeros_set, 1)
            nc.gpsimd.memset(earlier[:, :, :], 1.0).then_inc(zeros_set, 1)
            nc.gpsimd.memset(mix_w[:, :, :], 0.0).then_inc(zeros_set, 1)
            pool.wait_ge(zeros_set, 3)
            nc.gpsimd.affine_select(out=ident[:, :], in_=ident[:, :], compare_op=ALU.not_equal, fill=1.0,
                                    base=0, pattern=[[-1, P]], channel_multiplier=1).then_inc(consts_set, 1)
            nc.gpsimd.affine_select(out=earlier[:, :, :], in_=earlier[:, :, :], compare_op=ALU.is_gt, fill=0.0,
                                    base=0, pattern=[[1, E], [-1, E]], channel_multiplier=0).then_inc(consts_set, 1)
            pool.wait_ge(la_in, 16 * NC)
            la_v = lmix_w[:, :, :, :].rearrange("p c e r -> p c (e r)")
            nc.gpsimd.tensor_copy(w_hi[:, :, D:D + ER], la_v).then_inc(la_hi_set, 1)
            pool.wait_ge(la_hi_set, 1)
            nc.gpsimd.tensor_tensor(w_lo[:, :, D:D + ER], la_v, w_hi[:, :, D:D + ER].bitcast(f32),
                                    ALU.subtract).then_inc(la_lo_set, 1)
            pool.wait_ge(lb_in, 16)
            nc.gpsimd.tensor_copy(lb_hi[:, :], lb_raw[:, :]).then_inc(lb_hi_set, 1)
            pool.wait_ge(lb_hi_set, 1)
            nc.gpsimd.tensor_tensor(lb_lo[:, :], lb_raw[:, :], lb_hi[:, :].bitcast(f32),
                                    ALU.subtract).then_inc(lb_lo_set, 1)

        @block.tensor
        def _(pe):
            def transpose_w(g):
                pe.wait_ge(w_in[g], 16)
                for h in range(2):
                    if g >= 2:
                        pe.wait_ge(w_lo_set, 2 * (g - 2) + h + 1)
                    for j in range(HALF):
                        c = h * HALF + j
                        last = nc.tensor.transpose(acc[g % 2][h][:, j * P:(j + 1) * P],
                                                   w_stage[:, g, c * P:(c + 1) * P], ident[:, :])
                    last.then_inc(w_tr, 1)

            def mixing_kernels(n):
                if n >= 2:
                    pe.wait_ge(agg_act, 2 * (n - 1))
                    pe.wait_ge(agg_dve, 2 * (n - 1))
                for j in range(OG):
                    o = (OG * n + j) * PAR
                    last = nc.tensor.matmul(y_ps[n % 2][:, j * B:(j + 1) * B],
                                            mixk[:, o:o + PAR, :].rearrange("k o i -> k (o i)"), att_t[:, :],
                                            start=True, stop=True)
                last.then_inc(agg_mm, 1)

            pe.wait_ge(consts_set, 2)
            pe.wait_ge(cond_in, 16)
            nc.tensor.transpose(side[0][:, 0:P], cond_sb[:, :], ident[:, :]).then_inc(cond_on_pe, 1)
            transpose_w(0)
            pe.wait_ge(cond_t_ready, 1)
            pe.wait_ge(mlp_in, 16 * 6)
            nc.tensor.matmul(side[1][:, 0:P], w0_sb[:, :], cond_t[:, :], start=True, stop=True).then_inc(mlp_mm, 1)
            transpose_w(1)
            pe.wait_ge(mlp_act, 1)
            nc.tensor.matmul(side[0][:, 0:P], w1_sb[:, :], h1[:, :], start=True, stop=True).then_inc(mlp_mm, 1)
            transpose_w(2)
            pe.wait_ge(mlp_act, 2)
            nc.tensor.matmul(side[1][:, 0:K], h2[:, :], w2_sb[:, :], start=True, stop=True).then_inc(mlp_mm, 1)
            transpose_w(3)
            pe.wait_ge(att_step, 4)
            nc.tensor.transpose(side[0][0:K, 0:B], att[:, :], ident[:, :]).then_inc(att_tr, 1)
            pe.wait_ge(rw_in, 16)
            for c in range(NC):
                last = nc.tensor.transpose(side[1][:, c * E:(c + 1) * E], rw_raw[:, c * P:(c + 1) * P],
                                           ident[0:E, 0:E])
            last.then_inc(rw_tr, 1)
            pe.wait_ge(mix_in, 32)
            pe.wait_ge(att_t_ready, 1)
            nc.tensor.matmul(side[0][:, 0:C], att_t[:, :], bk_sb[:, :], start=True, stop=True).then_inc(bias_mm, 1)
            for n in range(NA):
                mixing_kernels(n)
                if n % 2 == 1:
                    transpose_w(4 + n // 2)

            def mix_chunk(t, k, c):
                h, j = c // HALF, c % HALF
                if c == 0:
                    pe.wait_ge(x_in[k], (t - k) * (16 // XR) + 16)
                    pe.wait_ge(mix_w_in[k], (t - k) * (MIX_W // XR) + MIX_W)
                if j == 0:
                    if isinstance(t, int) and t == 0:
                        pe.wait_ge(agg_act, PAR * NA)
                        pe.wait_ge(agg_dve, PAR * NA)
                    else:
                        pe.wait_ge(y_sum_ready, 2 * (t - 1) + h + 1)
                    if h == 1 and from_tile(t, 2):
                        pe.wait_ge(mid_hi_ready, t - 1)
                        pe.wait_ge(mid_lo_ready, t - 1)
                last = nc.tensor.matmul(y_ps[h][:, j * P:(j + 1) * P], x_sb[:, k, c * P:(c + 1) * P], mix_w[:, k, :],
                                        start=True, stop=True)
                if j == HALF - 1:
                    last.then_inc(mixed, 1)

            def main_chunk(t, k, c):
                s = k % 2
                if c % HALF == 0:
                    pe.wait_ge(y_hi_ready, 2 * t + c // HALF + 1)
                    pe.wait_ge(y_lo_ready, 2 * t + c // HALF + 1)
                if c == 0 and from_tile(t, 2):
                    pe.wait_ge(out_ready, 3 * (t - 2) + 3)
                cols = slice(c * P, (c + 1) * P)
                for y, w, first, final in ((y_hi, w_hi, True, False), (y_hi, w_lo, False, False),
                                           (y_lo, w_hi, False, True)):
                    for g, (a, z) in enumerate(GROUPS):
                        last = nc.tensor.matmul(acc[s][g][:, 0:z - a], y[:, s, cols], w[:, c, a:z],
                                                start=(c == 0 and first), stop=(c == NC - 1 and final))
                if c == NC - 1:
                    last.then_inc(main_done, 1)

            def transpose_mid(t, k):
                pe.wait_ge(route_step, ROUTE * t + ROUTE)
                pe.wait_ge(y_sum_ready, 2 * min(t + 1, NT - 1) + 2 if isinstance(t, int) else 2 * t + 4)
                nc.tensor.transpose(mid_ps, mid[:, :], ident[:, :]).then_inc(mid_tr, 1)

            def up(t, k):
                s = k % 2
                pe.wait_ge(mid_hi_ready, t + 1)
                pe.wait_ge(mid_lo_ready, t + 1)
                for m, w, final in ((mid_hi, lb_hi, False), (mid_hi, lb_lo, False), (mid_lo, lb_hi, True)):
                    for g, (a, z) in enumerate(GROUPS):
                        z = min(z, D)
                        last = nc.tensor.matmul(acc[s][g][:, 0:z - a], m[:, :], w[:, a:z], start=False, stop=final,
                                                skip_group_check=True)
                last.then_inc(up_done, 1)

            for c in range(NC):
                mix_chunk(0, 0, c)
            pe.wait_ge(w_hi_set, 2 * NC)
            pe.wait_ge(w_lo_set, 2 * NC)
            pe.wait_ge(rw_hi_set, 1)
            pe.wait_ge(rw_lo_set, 1)
            pe.wait_ge(la_lo_set, 1)
            pe.wait_ge(lb_lo_set, 1)

            def tile(t, k):
                for c in range(NC):
                    main_chunk(t, k, c)
                    if before_tile(t, NT - 1):
                        mix_chunk(t + 1, (k + 1) % XR, c)
                    if c == 2 and from_tile(t, 1):
                        transpose_mid(t - 1, (k - 1) % XR)
                    if c == 4 and from_tile(t, 1):
                        up(t - 1, (k - 1) % XR)

            over_tiles(pe, tile)
            transpose_mid(NT - 1, (NT - 1) % XR)
            up(NT - 1, (NT - 1) % XR)

        @block.scalar
        def _(act):
            act.dma_start(rw_raw[:, :], router_w).then_inc(rw_in, 16)
            for c in range(NC):
                act.dma_start(lmix_w[:, c, :, :],
                              lora_a[:, c * P:(c + 1) * P, :].rearrange("e p r -> p e r")).then_inc(la_in, 16)
            act.dma_start(lb_raw[:, :], lora_b.rearrange("e r d -> (e r) d")).then_inc(lb_in, 16)

            def take_w(g):
                for h in range(2):
                    act.wait_ge(w_tr, 2 * g + h + 1)
                    nc.scalar.activation(w_hi[:, h * HALF:(h + 1) * HALF, g * P:(g + 1) * P],
                                         acc[g % 2][h][:, :].rearrange("p (c n) -> p c n", c=HALF),
                                         ACT.Copy).then_inc(w_hi_set, 1)

            take_w(0)
            act.wait_ge(mlp_mm, 1)
            nc.scalar.activation(h1[:, :], side[1][:, 0:P], ACT.Gelu, bias=b0_sb[:, :]).then_inc(mlp_act, 1)
            take_w(1)
            act.wait_ge(mlp_mm, 2)
            nc.scalar.activation(h2[:, :], side[0][:, 0:P], ACT.Gelu, bias=b1_sb[:, :]).then_inc(mlp_act, 1)
            take_w(2)
            act.wait_ge(att_step, 2)
            nc.scalar.activation(exps[:, :], att[:, :], ACT.Exp, bias=att_nm[:, :],
                                 accum_out=att_sum[:, :]).then_inc(att_exp, 1)
            take_w(3)
            for n in range(NA):
                take_agg(act, nc.scalar.copy, agg_act, n, 0)
                if n % 2 == 1:
                    take_w(4 + n // 2)
            act.wait_ge(rw_tr, 1)
            nc.scalar.activation(w_hi[:, :, D + ER:NW], side[1][:, 0:NC * E].rearrange("p (c e) -> p c e", c=NC),
                                 ACT.Copy).then_inc(rw_hi_set, 1)

            def split_y(t, k, h):
                act.wait_ge(y_sum_ready, 2 * t + h + 1)
                if from_tile(t, 2):
                    act.wait_ge(main_done, t - 1)
                nc.scalar.activation(y_hi[:, k % 2, h * BANK:(h + 1) * BANK], y_sum[:, h, :],
                                     ACT.Copy).then_inc(y_hi_ready, 1)

            def exponents(t, k):
                act.wait_ge(route_step, ROUTE * t + 2)
                nc.scalar.activation(exps[:, :], logits[:, :], ACT.Exp, bias=neg_max[:, :]).then_inc(exps_ready, 1)

            def split_mid(t, k):
                act.wait_ge(mid_tr, t + 1)
                if from_tile(t, 1):
                    act.wait_ge(up_done, t)
                nc.scalar.activation(mid_hi[:, :], mid_ps, ACT.Copy).then_inc(mid_hi_ready, 1)

            split_y(0, 0, 0)

            def tile(t, k):
                if from_tile(t, 1):
                    exponents(t - 1, (k - 1) % XR)
                split_y(t, k, 1)
                if from_tile(t, 1):
                    split_mid(t - 1, (k - 1) % XR)
                if before_tile(t, NT - 1):
                    split_y(t + 1, (k + 1) % XR, 0)
                if from_tile(t, 1):
                    store(t - 1, (k - 1) % XR)

            def store(t, k):
                act.wait_ge(out_ready, 3 * t + 3)
                act.dma_start(out_t[t, :, :], out_sb[:, k % 2, :]).then_inc(out_stored[k % 2], 16)

            over_tiles(act, tile)
            exponents(NT - 1, (NT - 1) % XR)
            split_mid(NT - 1, (NT - 1) % XR)
            store(NT - 1, (NT - 1) % XR)
            for s in range(2):
                act.wait_ge(out_stored[s], 16 * (NT // 2))

        @block.vector
        def _(dve):
            def take_w(g):
                for h in range(2):
                    dve.wait_ge(w_hi_set, 2 * g + h + 1)
                    w = (slice(None), slice(h * HALF, (h + 1) * HALF), slice(g * P, (g + 1) * P))
                    nc.vector.tensor_tensor(w_lo[w], acc[g % 2][h][:, :].rearrange("p (c n) -> p c n", c=HALF),
                                            w_hi[w].bitcast(f32), ALU.subtract).then_inc(w_lo_set, 1)

            dve.wait_ge(cond_on_pe, 1)
            nc.vector.tensor_copy(cond_t[:, :], side[0][:, 0:P]).then_inc(cond_t_ready, 1)
            take_w(0)
            take_w(1)
            take_w(2)
            dve.wait_ge(mlp_mm, 3)
            nc.vector.tensor_tensor(att[:, :], side[1][:, 0:K], b2_sb[:, :], ALU.add).then_inc(att_step, 1)
            dve.wait_ge(att_step, 1)
            nc.vector.tensor_reduce(att_nm[:, :], att[:, :], AX.X, ALU.max, negate=True).then_inc(att_step, 1)
            dve.wait_ge(att_exp, 1)
            nc.vector.reciprocal(att_sum[:, :], att_sum[:, :]).then_inc(att_step, 1)
            dve.wait_ge(att_step, 3)
            nc.vector.tensor_scalar(att[:, :], exps[:, :], att_sum[:, :], None, ALU.mult).then_inc(att_step, 1)
            dve.wait_ge(att_tr, 1)
            nc.vector.tensor_copy(att_t[:, :], side[0][0:K, 0:B]).then_inc(att_t_ready, 1)
            take_w(3)
            dve.wait_ge(bias_mm, 1)
            nc.vector.tensor_copy(bias_rows[:, :], side[0][:, 0:C]).then_inc(bias_ready, 1)
            for n in range(NA):
                take_agg(dve, nc.vector.tensor_copy, agg_dve, n, 1)
                if n % 2 == 1:
                    take_w(4 + n // 2)
            dve.wait_ge(rw_hi_set, 1)
            rw = (slice(None), slice(None), slice(D + ER, NW))
            nc.vector.tensor_tensor(w_lo[rw], side[1][:, 0:NC * E].rearrange("p (c e) -> p c e", c=NC),
                                    w_hi[rw].bitcast(f32), ALU.subtract).then_inc(rw_lo_set, 1)

            def add_bias(t, k, h):
                if h == 0:
                    dve.wait_ge(mix_w_in[k], (t - k) * (MIX_W // XR) + MIX_W)
                dve.wait_ge(mixed, 2 * t + h + 1)
                nc.vector.tensor_tensor(y_sum[:, h, :].rearrange("p (c r) -> p c r", c=HALF),
                                        y_ps[h][:, :].rearrange("p (c r) -> p c r", c=HALF),
                                        bias_sb[:, k, :].unsqueeze(1).broadcast_to([P, HALF, P]),
                                        ALU.add).then_inc(y_sum_ready, 1)

            def split_y(t, k, h):
                dve.wait_ge(y_hi_ready, 2 * t + h + 1)
                cols = slice(h * BANK, (h + 1) * BANK)
                nc.vector.tensor_tensor(y_lo[:, k % 2, cols], y_sum[:, h, :], y_hi[:, k % 2, cols].bitcast(f32),
                                        ALU.subtract).then_inc(y_lo_ready, 1)

            def route_logits(t, k):
                dve.wait_ge(main_done, t + 1)
                nc.vector.tensor_copy(logits[:, :], side[k % 2][:, SIDE + ER:SIDE + ER + E]).then_inc(route_step, 1)
                dve.wait_ge(route_step, ROUTE * t + 1)
                nc.vector.tensor_reduce(neg_max[:, :], logits[:, :], AX.X, ALU.max, negate=True).then_inc(route_step, 1)

            def route_choice(t, k):
                other = logits[:, :].unsqueeze(1).broadcast_to([P, E, E])
                own = logits[:, :].unsqueeze(2).broadcast_to([P, E, E])
                nc.vector.tensor_tensor(beats[:, :, 0:E], other, own, ALU.is_gt).then_inc(route_step, 1)
                nc.vector.tensor_tensor(ties[:, :, :], other, own, ALU.is_equal).then_inc(route_step, 1)
                dve.wait_ge(route_step, ROUTE * t + 4)
                nc.vector.tensor_tensor(beats[:, :, E:2 * E], ties[:, :, :], earlier[:, :, :],
                                        ALU.mult).then_inc(route_step, 1)
                dve.wait_ge(route_step, ROUTE * t + 5)
                nc.vector.tensor_reduce(rank[:, :], beats[:, :, :], AX.X, ALU.add).then_inc(route_step, 1)
                dve.wait_ge(route_step, ROUTE * t + 6)
                nc.vector.tensor_scalar(chosen[:, :], rank[:, :], float(TOP), None, ALU.is_lt).then_inc(route_step, 1)

            def route_weigh(t, k):
                dve.wait_ge(route_step, ROUTE * t + 7)
                dve.wait_ge(exps_ready, t + 1)
                nc.vector.tensor_tensor(picked[:, :], exps[:, :], chosen[:, :], ALU.mult).then_inc(route_step, 1)
                dve.wait_ge(route_step, ROUTE * t + 8)
                nc.vector.tensor_reduce(total[:, :], picked[:, :], AX.X, ALU.add).then_inc(route_step, 1)
                dve.wait_ge(route_step, ROUTE * t + 9)
                nc.vector.reciprocal(inv_total[:, :], total[:, :]).then_inc(route_step, 1)
                dve.wait_ge(route_step, ROUTE * t + 10)
                nc.vector.tensor_scalar(gate[:, :], picked[:, :], inv_total[:, :], SCALING,
                                        ALU.mult, ALU.mult).then_inc(route_step, 1)
                dve.wait_ge(route_step, ROUTE * t + 11)
                if from_tile(t, 1):
                    dve.wait_ge(mid_tr, t)
                nc.vector.tensor_tensor(mid[:, :].rearrange("p (e r) -> p e r", e=E),
                                        side[k % 2][:, MID].rearrange("p (e r) -> p e r", e=E),
                                        gate[:, :].unsqueeze(2).broadcast_to([P, E, R]),
                                        ALU.mult).then_inc(route_step, 1)

            def split_mid(t, k):
                dve.wait_ge(mid_hi_ready, t + 1)
                nc.vector.tensor_tensor(mid_lo[:, :], mid_ps, mid_hi[:, :].bitcast(f32),
                                        ALU.subtract).then_inc(mid_lo_ready, 1)

            def add_x(t, k):
                dve.wait_ge(up_done, t + 1)
                if from_tile(t, 2):
                    dve.wait_ge(out_stored[k % 2], 8 * (t - k % 2))
                for g, (a, z) in enumerate(GROUPS):
                    z = min(z, D)
                    nc.vector.tensor_tensor(out_sb[:, k % 2, a:z], acc[k % 2][g][:, 0:z - a], x_sb[:, k, a:z],
                                            ALU.add).then_inc(out_ready, 1)

            add_bias(0, 0, 0)
            split_y(0, 0, 0)

            def tile(t, k):
                if from_tile(t, 1):
                    route_logits(t - 1, (k - 1) % XR)
                add_bias(t, k, 1)
                if from_tile(t, 1):
                    route_choice(t - 1, (k - 1) % XR)
                    route_weigh(t - 1, (k - 1) % XR)
                split_y(t, k, 1)
                if from_tile(t, 1):
                    split_mid(t - 1, (k - 1) % XR)
                if before_tile(t, NT - 1):
                    add_bias(t + 1, (k + 1) % XR, 0)
                    split_y(t + 1, (k + 1) % XR, 0)
                if from_tile(t, 1):
                    add_x(t - 1, (k - 1) % XR)

            over_tiles(dve, tile)
            last = (NT - 1, (NT - 1) % XR)
            route_logits(*last)
            route_choice(*last)
            route_weigh(*last)
            split_mid(*last)
            add_x(*last)

    return nc


_INS = ['x', 'cond_128', 'L0_cond_W0', 'L0_cond_b0', 'L0_cond_W1', 'L0_cond_b1', 'L0_cond_W2', 'L0_cond_b2',
        'L0_cond_weight', 'L0_cond_bias_k', 'L0_ffn_base_W', 'L0_ffn_router_W', 'L0_ffn_lora_A', 'L0_ffn_lora_B']


def kernel(**inputs):
    import numpy as np
    import concourse.bacc as bacc
    from concourse.bass_utils import run_bass_kernel_spmd

    nc = bacc.Bacc("TRN2", target_bir_lowering=False, num_devices=1)
    arrays, args = {}, []
    for name in _INS:
        a = np.ascontiguousarray(inputs[name])
        arrays[f"in_{name}"] = a
        args.append(nc.dram_tensor(f"in_{name}", a.shape, mybir.dt.from_np(a.dtype), kind="ExternalInput").ap())
    shape = inputs['x'].shape
    args.append(nc.dram_tensor("out", shape, mybir.dt.float32, kind="ExternalOutput").ap())
    adaln_ffn_kernel(nc, *args)
    r = run_bass_kernel_spmd(nc, [arrays], core_ids=[0])
    return r.results[0]["out"]
```

```python
import concourse.bass as bass
from concourse import mybir
from contextlib import ExitStack


def adaln_ffn_kernel(nc, x, cond, w0, b0, w1, b1, w2, b2, weight, bias_k, base_w, router_w, lora_a, lora_b, out):
    f32, f32r = mybir.dt.float32, mybir.dt.float32r
    ALU, ACT, AX = mybir.AluOpType, mybir.ActivationFunctionType, mybir.AxisListType

    B, C, D = x.shape
    P = 128
    PAR = P // C
    NT = B // PAR
    NC = D // P
    K = weight.shape[0]
    E, _, R = lora_a.shape
    ER = E * R
    NW = D + ER + E
    GW = -(-NW // 3 // 4) * 4
    GROUPS = [(0, GW), (GW, 2 * GW), (2 * GW, NW)]
    SIDE = D - 2 * GW
    SCALING = 32 / 16
    BANK = 512
    HALF = NC // 2
    XR = 4
    TOP = 2
    OG = BANK // B
    NA = C // PAR // OG
    Q = 32
    W_AFTER_AGG = {1: 2, 2: 3, 3: 4, 4: 5, 5: 6}
    W_AFTER_ALL = range(2 + len(W_AFTER_AGG), D // P)
    MK = 4

    x_t = x.rearrange("(t b) c d -> t (b c) d", b=PAR)
    out_t = out.rearrange("(t b) c d -> t (b c) d", b=PAR)
    bias_dram = nc.dram_tensor("bias_rows", [NT, PAR * C], f32)

    ctx = ExitStack()
    with ctx:
        def sb(name, shape, dt=f32):
            return ctx.enter_context(nc.sbuf_tensor(name, shape, dt))

        def sem(name):
            return ctx.enter_context(nc.semaphore(name))

        w_hi = sb("w_hi", [P, NC, NW], f32r)
        w_lo = sb("w_lo", [P, NC, NW], f32r)
        lb_hi = sb("lb_hi", [ER, D], f32r)
        lb_lo = sb("lb_lo", [ER, D], f32r)
        agg = sb("agg", [P, NT, C])
        x_sb = sb("x_sb", [P, XR, D])
        bias_sb = sb("bias_sb", [P, XR, P])
        mix_w = sb("mix_w", [P, XR, P])
        y_sum = sb("y_sum", [P, 2, BANK])
        y_hi = sb("y_hi", [P, 2, D], f32r)
        y_lo = sb("y_lo", [P, 2, D], f32r)
        out_sb = sb("out_sb", [P, 2, D])
        logits = sb("logits", [P, E])
        neg_max = sb("neg_max", [P, 1])
        beats = sb("beats", [P, E, 2 * E])
        ties = sb("ties", [P, E, E])
        earlier = sb("earlier", [P, E, E])
        rank = sb("rank", [P, E])
        chosen = sb("chosen", [P, E])
        exps = sb("exps", [P, E])
        picked = sb("picked", [P, E])
        total = sb("total", [P, 1])
        inv_total = sb("inv_total", [P, 1])
        gate = sb("gate", [P, E])
        mid = sb("mid", [P, ER])
        mid_hi = sb("mid_hi", [ER, P], f32r)
        mid_lo = sb("mid_lo", [ER, P], f32r)
        w_stage = sb("w_stage", [P, D // P, D])
        la_raw = sb("la_raw", [P, NC, E, R])
        lb_raw = out_sb[:, 0, :]
        rw_raw = out_sb[0:E, 1, :]
        mixk_raw = x_sb[:, :, :].rearrange("p s d -> p (s d)")
        mixk = sb("mixk", [P, C * C], f32r)
        att_rep = sb("att_rep", [P, P])
        att_parts = sb("att_parts", [P, B], f32r)
        ident = sb("ident", [P, P])
        warm = sb("warm", [P, 1])
        cond_sb = sb("cond_sb", [P, P])
        cond_t = sb("cond_t", [P, P])
        w0_sb, w1_sb = sb("w0_sb", [P, P]), sb("w1_sb", [P, P])
        w2_sb = sb("w2_sb", [P, K])
        b0_sb, b1_sb = sb("b0_sb", [P, 1]), sb("b1_sb", [P, 1])
        b2_sb = sb("b2_sb", [P, K])
        h1, h2 = sb("h1", [P, P]), sb("h2", [P, P])
        att = sb("att", [P, K])
        att_nm = sb("att_nm", [P, 1])
        att_sum = sb("att_sum", [P, 1])
        att_t = sb("att_t", [K, B])
        bk_sb = sb("bk_sb", [K, C])
        bias_rows = sb("bias_rows_sb", [B, C])

        acc = [[ctx.enter_context(nc.psum_tensor(f"acc{s}{h}", [P, BANK], f32)) for h in range(3)] for s in range(2)]
        y_ps = [ctx.enter_context(nc.psum_tensor(f"y_ps{h}", [P, BANK], f32)) for h in range(2)]
        side = [acc[s][2] for s in range(2)]
        MID = slice(SIDE, SIDE + ER)
        mid_ps = y_ps[1][:, 0:P]

        cond_in, mix_in, bk_in, rw_in, la_in, lb_in = (sem(n) for n in (
            "cond_in", "mix_in", "bk_in", "rw_in", "la_in", "lb_in"))
        mlp_in = [sem(f"mlp_in{n}") for n in range(3)]
        w_in = [sem(f"w_in{s}") for s in range(D // P)]
        zeros_set, consts_set = sem("zeros_set"), sem("consts_set")
        cond_on_pe, cond_t_ready = sem("cond_on_pe"), sem("cond_t_ready")
        mlp_mm, mlp_act, att_step, att_exp = sem("mlp_mm"), sem("mlp_act"), sem("att_step"), sem("att_exp")
        att_tr, att_t_ready, bias_mm, bias_ready, bias_out = (sem(n) for n in (
            "att_tr", "att_t_ready", "bias_mm", "bias_ready", "bias_out"))
        w_tr, w_hi_set, w_lo_set = sem("w_tr"), sem("w_hi_set"), sem("w_lo_set")
        rw_tr, rw_hi_set, rw_lo_set = sem("rw_tr"), sem("rw_hi_set"), sem("rw_lo_set")
        la_hi_set, la_lo_set, lb_hi_set, lb_lo_set = (sem(n) for n in (
            "la_hi_set", "la_lo_set", "lb_hi_set", "lb_lo_set"))
        mixk_zero, mixk_hi_set, mixk_set, mixk_pool_hi_set, mixk_pool_set = (sem(n) for n in (
            "mixk_zero", "mixk_hi_set", "mixk_set", "mixk_pool_hi_set", "mixk_pool_set"))
        att_hi_set, att_lo_set = sem("att_hi_set"), sem("att_lo_set")
        agg_mm, agg_act, agg_dve = sem("agg_mm"), sem("agg_act"), sem("agg_dve")
        x_in = [sem(f"x_in{s}") for s in range(XR)]
        mix_w_in = [sem(f"mix_w_in{s}") for s in range(XR)]
        MIX_W = 16 * (PAR + 1)
        mixed, y_sum_ready, y_hi_ready, y_lo_ready = (sem(n) for n in (
            "mixed", "y_sum_ready", "y_hi_ready", "y_lo_ready"))
        main_done, route_step, exps_ready, mid_tr, mid_hi_ready, mid_lo_ready = (sem(n) for n in (
            "main_done", "route_step", "exps_ready", "mid_tr", "mid_hi_ready", "mid_lo_ready"))
        up_done, out_ready = sem("up_done"), sem("out_ready")
        out_stored = [sem(f"out_stored{s}") for s in range(2)]

        ROUTE = 12

        def from_tile(t, n):
            return t >= n if isinstance(t, int) else True

        def before_tile(t, n):
            return t < n if isinstance(t, int) else True

        def over_tiles(eng, body):
            for t in range(XR):
                body(t, t)
            with eng.Fori(1, NT // XR - 1) as i:
                for k in range(XR):
                    body(i * XR + k, k)
            for t in range(NT - XR, NT):
                body(t, t % XR)

        def mixk_piece(m):
            return slice(m * C * C // MK, (m + 1) * C * C // MK)

        def agg_out(eng, n):
            eng.wait_ge(agg_act, PAR * (n + (n + 1) // 2))
            if n > 1:
                eng.wait_ge(agg_dve, PAR * (n // 2))

        def take_agg(copy, n, o, taken):
            for b in range(PAR):
                src = y_ps[n % 2][o * C:(o + 1) * C, :].rearrange("i (j t b) -> i b t j", j=OG, b=PAR)
                dst = agg[b * C:(b + 1) * C, :, :].rearrange("i t (n j o) -> i n o t j", j=OG, o=PAR)
                copy(dst[:, n, o, :, :], src[:, b, :, :]).then_inc(taken, 1)

        block = ctx.enter_context(nc.Block())

        @block.sync
        def _(sp):
            sp.dma_start(cond_sb[:, :], cond).then_inc(cond_in, 16)
            sp.dma_start(w0_sb[:, :], w0).then_inc(mlp_in[0], 16)
            sp.dma_start(b0_sb[:, :], b0.rearrange("(p a) -> p a", a=1)).then_inc(mlp_in[0], 16)
            sp.dma_start(w1_sb[:, :], w1).then_inc(mlp_in[1], 16)
            sp.dma_start(b1_sb[:, :], b1.rearrange("(p a) -> p a", a=1)).then_inc(mlp_in[1], 16)
            sp.dma_start(w2_sb[:, :], w2).then_inc(mlp_in[2], 16)
            sp.dma_start(b2_sb[:, :], b2.partition_broadcast(P)).then_inc(mlp_in[2], 16)
            sp.dma_start(bk_sb[:, :], bias_k).then_inc(bk_in, 16)
            for g in range(D // P):
                sp.dma_start(w_stage[:, g, :], base_w[g * P:(g + 1) * P, :]).then_inc(w_in[g], 16)
                if g == 0:
                    sp.wait_ge(mixk_zero, 2)
                    for q in range(P // Q):
                        sp.dma_start(mixk_raw[q * Q:q * Q + K, :],
                                     weight.rearrange("k o i a -> k (o i a)")).then_inc(mix_in, 16)
            sp.dma_start(rw_raw[:, :], router_w).then_inc(rw_in, 16)
            for c in range(NC):
                sp.dma_start(la_raw[:, c, :, :],
                             lora_a[:, c * P:(c + 1) * P, :].rearrange("e p r -> p e r")).then_inc(la_in, 16)

            def mixing_weights(t, k):
                for b in range(PAR):
                    part = slice(b * C, (b + 1) * C)
                    sp.dma_start(mix_w[part, k, part], agg[part, t, :]).then_inc(mix_w_in[k], 16)
                sp.dma_start(bias_sb[:, k, :], bias_dram[t, :].partition_broadcast(P)).then_inc(mix_w_in[k], 16)

            def load(t, k):
                sp.wait_ge(out_ready, 3 * (t - XR) + 3)
                sp.dma_start(x_sb[:, k, :], x_t[t, :, :]).then_inc(x_in[k], 16)
                mixing_weights(t, k)

            sp.wait_ge(bias_ready, 1)
            sp.dma_start(bias_dram.rearrange("t (b c) -> (t b) c", b=PAR), bias_rows[:, :]).then_inc(bias_out, 16)
            sp.wait_ge(mixk_set, MK // 2)
            sp.wait_ge(mixk_pool_set, MK // 2)
            sp.dma_start(x_sb[:, 0, :], x_t[0, :, :]).then_inc(x_in[0], 16)
            sp.dma_start(lb_raw[:, :], lora_b.rearrange("e r d -> (e r) d")).then_inc(lb_in, 16)
            sp.wait_ge(bias_out, 16)
            sp.dma_start(bias_sb[:, 0, :], bias_dram[0, :].partition_broadcast(P)).then_inc(mix_w_in[0], 16)
            agg_out(sp, NA)
            sp.wait_ge(zeros_set, 4)
            for k in range(1, XR):
                sp.dma_start(x_sb[:, k, :], x_t[k, :, :]).then_inc(x_in[k], 16)
                mixing_weights(k, k)
            with sp.Fori(1, NT // XR) as i:
                for k in range(XR):
                    load(i * XR + k, k)

        @block.gpsimd
        def _(pool):
            nc.gpsimd.memset(ident[:, :], 0.0).then_inc(zeros_set, 1)
            nc.gpsimd.memset(earlier[:, :, :], 1.0).then_inc(zeros_set, 1)
            pool.wait_ge(zeros_set, 2)
            nc.gpsimd.affine_select(out=ident[:, :], in_=ident[:, :], compare_op=ALU.not_equal, fill=1.0,
                                    base=0, pattern=[[-1, P]], channel_multiplier=1).then_inc(consts_set, 1)
            nc.gpsimd.affine_select(out=earlier[:, :, :], in_=earlier[:, :, :], compare_op=ALU.is_gt, fill=0.0,
                                    base=0, pattern=[[1, E], [-1, E]], channel_multiplier=0).then_inc(consts_set, 1)
            nc.gpsimd.memset(mixk_raw[:, C * C // 2:], 0.0).then_inc(mixk_zero, 1)
            nc.gpsimd.memset(att_rep[:, :], 0.0).then_inc(zeros_set, 1)
            nc.gpsimd.memset(mix_w[:, :, :], 0.0).then_inc(zeros_set, 1)
            pool.wait_ge(mix_in, 16 * P // Q)
            for m in range(MK // 2, MK):
                cols = mixk_piece(m)
                if m > MK // 2:
                    pool.wait_ge(mixk_pool_set, m - MK // 2)
                nc.gpsimd.tensor_copy(mixk[:, cols], mixk_raw[:, cols]).then_inc(mixk_pool_hi_set, 1)
                pool.wait_ge(mixk_pool_hi_set, m - MK // 2 + 1)
                nc.gpsimd.tensor_tensor(mixk[2 * Q:, cols], mixk_raw[2 * Q:, cols], mixk[2 * Q:, cols].bitcast(f32),
                                        ALU.subtract).then_inc(mixk_pool_set, 1)
            pool.wait_ge(mixk_pool_set, MK // 2)
            pool.wait_ge(la_in, 16 * NC)
            nc.gpsimd.tensor_copy(w_hi[:, :, D:D + ER],
                                  la_raw[:, :, :, :].rearrange("p c e r -> p c (e r)")).then_inc(la_hi_set, 1)
            pool.wait_ge(la_hi_set, 1)
            nc.gpsimd.tensor_tensor(w_lo[:, :, D:D + ER], la_raw[:, :, :, :].rearrange("p c e r -> p c (e r)"),
                                    w_hi[:, :, D:D + ER].bitcast(f32), ALU.subtract).then_inc(la_lo_set, 1)
            pool.wait_ge(lb_in, 16)
            nc.gpsimd.tensor_copy(lb_hi[:, :], lb_raw[:, :]).then_inc(lb_hi_set, 1)
            pool.wait_ge(lb_hi_set, 1)
            nc.gpsimd.tensor_tensor(lb_lo[:, :], lb_raw[:, :], lb_hi[:, :].bitcast(f32),
                                    ALU.subtract).then_inc(lb_lo_set, 1)

        @block.tensor
        def _(pe):
            def transpose_w(g):
                pe.wait_ge(w_in[g], 16)
                for h in range(2):
                    if g >= 2:
                        pe.wait_ge(w_lo_set, 2 * (g - 2) + h + 1)
                    for j in range(HALF):
                        c = h * HALF + j
                        last = nc.tensor.transpose(acc[g % 2][h][:, j * P:(j + 1) * P],
                                                   w_stage[:, g, c * P:(c + 1) * P], ident[:, :])
                    last.then_inc(w_tr, 1)

            def mixing_kernels(n):
                m = n * MK // NA
                if m < MK // 2:
                    pe.wait_ge(mixk_set, m + 1)
                else:
                    pe.wait_ge(mixk_pool_set, m - MK // 2 + 1)
                if n >= 2:
                    agg_out(pe, n - 1)
                for j in range(OG):
                    o = (OG * n + j) * PAR * C
                    last = nc.tensor.matmul(y_ps[n % 2][:, j * B:(j + 1) * B], mixk[:, o:o + PAR * C],
                                            att_parts[:, :], start=True, stop=True)
                last.then_inc(agg_mm, 1)

            pe.wait_ge(consts_set, 2)
            pe.wait_ge(cond_in, 16)
            nc.tensor.transpose(side[0][:, 0:P], cond_sb[:, :], ident[:, :]).then_inc(cond_on_pe, 1)
            pe.wait_ge(cond_t_ready, 1)
            pe.wait_ge(mlp_in[0], 32)
            nc.tensor.matmul(side[1][:, 0:P], w0_sb[:, :], cond_t[:, :], start=True, stop=True).then_inc(mlp_mm, 1)
            pe.wait_ge(mlp_act, 1)
            pe.wait_ge(mlp_in[1], 32)
            nc.tensor.matmul(side[0][:, 0:P], w1_sb[:, :], h1[:, :], start=True, stop=True).then_inc(mlp_mm, 1)
            pe.wait_ge(mlp_act, 2)
            pe.wait_ge(mlp_in[2], 32)
            nc.tensor.matmul(side[1][:, 0:K], h2[:, :], w2_sb[:, :], start=True, stop=True).then_inc(mlp_mm, 1)
            transpose_w(0)
            pe.wait_ge(att_step, 4)
            nc.tensor.transpose(side[0][:, 0:B], att_rep[:, :], ident[:, :]).then_inc(att_tr, 1)
            transpose_w(1)
            pe.wait_ge(bk_in, 16)
            pe.wait_ge(att_t_ready, 1)
            pe.wait_ge(att_lo_set, 2)
            nc.tensor.matmul(side[0][:, 0:C], att_t[:, :], bk_sb[:, :], start=True, stop=True).then_inc(bias_mm, 1)
            for n in range(NA):
                mixing_kernels(n)
                if n in W_AFTER_AGG:
                    transpose_w(W_AFTER_AGG[n])
            for g in W_AFTER_ALL:
                transpose_w(g)
            pe.wait_ge(rw_in, 16)
            for c in range(NC):
                last = nc.tensor.transpose(side[1][:, c * E:(c + 1) * E], rw_raw[:, c * P:(c + 1) * P],
                                           ident[0:E, 0:E])
            last.then_inc(rw_tr, 1)

            def mix_chunk(t, k, c):
                h, j = c // HALF, c % HALF
                if c == 0:
                    pe.wait_ge(x_in[k], (t - k) * (16 // XR) + 16)
                    pe.wait_ge(mix_w_in[k], (t - k) * (MIX_W // XR) + MIX_W)
                if j == 0:
                    if isinstance(t, int) and t == 0:
                        agg_out(pe, NA)
                    else:
                        pe.wait_ge(y_sum_ready, 2 * (t - 1) + h + 1)
                    if h == 1 and from_tile(t, 2):
                        pe.wait_ge(mid_hi_ready, t - 1)
                        pe.wait_ge(mid_lo_ready, t - 1)
                last = nc.tensor.matmul(y_ps[h][:, j * P:(j + 1) * P], x_sb[:, k, c * P:(c + 1) * P], mix_w[:, k, :],
                                        start=True, stop=True)
                if j == HALF - 1:
                    last.then_inc(mixed, 1)

            def main_chunk(t, k, c):
                if c % HALF == 0:
                    pe.wait_ge(y_hi_ready, 2 * t + c // HALF + 1)
                    pe.wait_ge(y_lo_ready, 2 * t + c // HALF + 1)
                if isinstance(t, int) and t == 0 and c == HALF:
                    pe.wait_ge(w_lo_set, 2 * NC)
                if c == 0 and from_tile(t, 2):
                    pe.wait_ge(out_ready, 3 * (t - 2) + 3)
                last = main_products(k, c, range(3))
                if c == NC - 1:
                    last.then_inc(main_done, 1)

            def main_products(k, c, groups):
                s = k % 2
                for y, w, first, final in ((y_hi, w_hi, True, False), (y_hi, w_lo, False, False),
                                           (y_lo, w_hi, False, True)):
                    for g in groups:
                        a, z = GROUPS[g]
                        last = nc.tensor.matmul(acc[s][g][:, 0:z - a], y[:, s, c * P:(c + 1) * P], w[:, c, a:z],
                                                start=(c == 0 and first), stop=(c == NC - 1 and final))
                return last

            def transpose_mid(t, k):
                pe.wait_ge(route_step, ROUTE * t + ROUTE)
                pe.wait_ge(y_sum_ready, 2 * min(t + 1, NT - 1) + 2 if isinstance(t, int) else 2 * t + 4)
                nc.tensor.transpose(mid_ps, mid[:, :], ident[:, :]).then_inc(mid_tr, 1)

            def up(t, k):
                pe.wait_ge(mid_hi_ready, t + 1)
                pe.wait_ge(mid_lo_ready, t + 1)
                if isinstance(t, int) and t == 0:
                    pe.wait_ge(lb_lo_set, 1)
                for g in range(3):
                    up_group(k, g)

            def up_group(k, g):
                a, z = GROUPS[g][0], min(GROUPS[g][1], D)
                for m, w, final in ((mid_hi, lb_hi, False), (mid_hi, lb_lo, False), (mid_lo, lb_hi, True)):
                    last = nc.tensor.matmul(acc[k % 2][g][:, 0:z - a], m[:, :], w[:, a:z], start=False, stop=final,
                                            skip_group_check=True)
                last.then_inc(up_done, 1)

            for c in range(NC):
                mix_chunk(0, 0, c)
            pe.wait_ge(w_lo_set, 2 * NC - 1)
            pe.wait_ge(rw_hi_set, 1)
            pe.wait_ge(rw_lo_set, 1)
            pe.wait_ge(la_lo_set, 1)

            def tile(t, k):
                if isinstance(t, int) and t == NT - 1:
                    return last_tile(t, k)
                for c in range(NC):
                    main_chunk(t, k, c)
                    mix_chunk(t + 1, (k + 1) % XR, c)
                    if c == 2 and from_tile(t, 1):
                        transpose_mid(t - 1, (k - 1) % XR)
                    if c == 4 and from_tile(t, 1):
                        up(t - 1, (k - 1) % XR)

            def last_tile(t, k):
                pe.wait_ge(out_ready, 3 * (t - 2) + 3)
                first, second = range(HALF), range(HALF, NC)
                for g, chunks in ((2, first), (1, first), (2, second), (1, second), (0, first), (0, second)):
                    if g == 2:
                        pe.wait_ge(y_hi_ready, 2 * t + chunks[0] // HALF + 1)
                        pe.wait_ge(y_lo_ready, 2 * t + chunks[0] // HALF + 1)
                    for c in chunks:
                        last = main_products(k, c, (g,))
                    if (g, chunks) == (1, first):
                        transpose_mid(t - 1, (k - 1) % XR)
                    if (g, chunks) == (2, second):
                        last.then_inc(main_done, 1)
                        up(t - 1, (k - 1) % XR)
                    if (g, chunks) == (0, first):
                        transpose_mid(t, k)
                pe.wait_ge(mid_hi_ready, t + 1)
                pe.wait_ge(mid_lo_ready, t + 1)
                for g in (2, 1, 0):
                    up_group(k, g)

            over_tiles(pe, tile)

        @block.scalar
        def _(act):
            nc.scalar.activation(warm[:, :], nc.const_aps.tensor(0.0, (P, 1)), ACT.Gelu)

            def take_w(g):
                for h in range(2):
                    act.wait_ge(w_tr, 2 * g + h + 1)
                    nc.scalar.activation(w_hi[:, h * HALF:(h + 1) * HALF, g * P:(g + 1) * P],
                                         acc[g % 2][h][:, :].rearrange("p (c n) -> p c n", c=HALF),
                                         ACT.Copy).then_inc(w_hi_set, 1)

            act.wait_ge(mlp_mm, 1)
            nc.scalar.activation(h1[:, :], side[1][:, 0:P], ACT.Gelu, bias=b0_sb[:, :]).then_inc(mlp_act, 1)
            act.wait_ge(mlp_mm, 2)
            nc.scalar.activation(h2[:, :], side[0][:, 0:P], ACT.Gelu, bias=b1_sb[:, :]).then_inc(mlp_act, 1)
            nc.scalar.activation(warm[:, :], nc.const_aps.tensor(0.0, (P, 1)), ACT.Exp)
            act.wait_ge(att_step, 2)
            nc.scalar.activation(exps[:, :], att[:, :], ACT.Exp, bias=att_nm[:, :],
                                 accum_out=att_sum[:, :]).then_inc(att_exp, 1)

            def mixk_high(m):
                nc.scalar.activation(mixk[:, mixk_piece(m)], mixk_raw[:, mixk_piece(m)],
                                     ACT.Copy).then_inc(mixk_hi_set, 1)

            act.wait_ge(mix_in, 16 * P // Q)
            mixk_high(0)
            take_w(0)
            act.wait_ge(att_tr, 1)
            nc.scalar.activation(att_parts[:, :], side[0][:, 0:B], ACT.Copy).then_inc(att_hi_set, 1)
            mixk_high(1)
            take_w(1)

            for n in range(NA):
                act.wait_ge(agg_mm, n + 1)
                take_agg(nc.scalar.copy, n, 0, agg_act)
                if n % 2 == 0:
                    take_agg(nc.scalar.copy, n, 1, agg_act)
                if n in W_AFTER_AGG:
                    take_w(W_AFTER_AGG[n])
            agg_out(act, NA)
            act.wait_ge(zeros_set, 4)
            for b in range(PAR):
                part = slice(b * C, (b + 1) * C)
                nc.scalar.copy(mix_w[part, 0, part], agg[part, 0, :]).then_inc(mix_w_in[0], 16)
            for g in W_AFTER_ALL:
                take_w(g)
            act.wait_ge(rw_tr, 1)
            nc.scalar.activation(w_hi[:, :, D + ER:NW], side[1][:, 0:NC * E].rearrange("p (c e) -> p c e", c=NC),
                                 ACT.Copy).then_inc(rw_hi_set, 1)

            def split_y(t, k, h):
                act.wait_ge(y_sum_ready, 2 * t + h + 1)
                if from_tile(t, 2):
                    act.wait_ge(main_done, t - 1)
                nc.scalar.activation(y_hi[:, k % 2, h * BANK:(h + 1) * BANK], y_sum[:, h, :],
                                     ACT.Copy).then_inc(y_hi_ready, 1)

            def exponents(t, k):
                act.wait_ge(route_step, ROUTE * t + 2)
                nc.scalar.activation(exps[:, :], logits[:, :], ACT.Exp, bias=neg_max[:, :]).then_inc(exps_ready, 1)

            def split_mid(t, k):
                act.wait_ge(mid_tr, t + 1)
                if from_tile(t, 1):
                    act.wait_ge(up_done, 3 * t)
                nc.scalar.activation(mid_hi[:, :], mid_ps, ACT.Copy).then_inc(mid_hi_ready, 1)

            split_y(0, 0, 0)

            def tile(t, k):
                if from_tile(t, 1):
                    exponents(t - 1, (k - 1) % XR)
                split_y(t, k, 1)
                if from_tile(t, 1):
                    split_mid(t - 1, (k - 1) % XR)
                if before_tile(t, NT - 1):
                    split_y(t + 1, (k + 1) % XR, 0)
                if isinstance(t, int) and t == NT - 1:
                    exponents(t, k)
                if from_tile(t, 1):
                    store(t - 1, (k - 1) % XR)

            def store(t, k):
                act.wait_ge(out_ready, 3 * t + 3)
                act.dma_start(out_t[t, :, :], out_sb[:, k % 2, :]).then_inc(out_stored[k % 2], 16)

            over_tiles(act, tile)
            split_mid(NT - 1, (NT - 1) % XR)
            for n, g in enumerate((2, 1, 0)):
                a, z = GROUPS[g][0], min(GROUPS[g][1], D)
                act.wait_ge(out_ready, 3 * (NT - 1) + n + 1)
                act.dma_start(out_t[NT - 1, :, a:z], out_sb[:, (NT - 1) % 2, a:z]).then_inc(out_stored[1], 16)
            act.wait_ge(out_stored[0], 16 * (NT // 2))
            act.wait_ge(out_stored[1], 16 * (NT // 2 - 1 + 3))

        @block.vector
        def _(dve):
            def take_w(g):
                for h in range(2):
                    dve.wait_ge(w_hi_set, 2 * g + h + 1)
                    w = (slice(None), slice(h * HALF, (h + 1) * HALF), slice(g * P, (g + 1) * P))
                    nc.vector.tensor_tensor(w_lo[w], acc[g % 2][h][:, :].rearrange("p (c n) -> p c n", c=HALF),
                                            w_hi[w].bitcast(f32), ALU.subtract).then_inc(w_lo_set, 1)

            nc.vector.memset(mixk_raw[:, :C * C // 2], 0.0).then_inc(mixk_zero, 1)
            dve.wait_ge(cond_on_pe, 1)
            nc.vector.tensor_copy(cond_t[:, :], side[0][:, 0:P]).then_inc(cond_t_ready, 1)
            dve.wait_ge(mlp_mm, 3)
            nc.vector.tensor_tensor(att[:, :], side[1][:, 0:K], b2_sb[:, :], ALU.add).then_inc(att_step, 1)
            dve.wait_ge(att_step, 1)
            nc.vector.tensor_reduce(att_nm[:, :], att[:, :], AX.X, ALU.max, negate=True).then_inc(att_step, 1)
            dve.wait_ge(att_exp, 1)
            nc.vector.reciprocal(att_sum[:, :], att_sum[:, :]).then_inc(att_step, 1)
            dve.wait_ge(att_step, 3)
            dve.wait_ge(zeros_set, 3)
            nc.vector.tensor_scalar(att_rep[:, :].rearrange("b (q k) -> b q k", k=Q)[:, :, 0:K],
                                    exps[:, :].unsqueeze(1).broadcast_to([B, P // Q, K]), att_sum[:, :], None,
                                    ALU.mult).then_inc(att_step, 1)

            def mixk_low(m):
                cols = mixk_piece(m)
                dve.wait_ge(mixk_hi_set, m + 1)
                nc.vector.tensor_tensor(mixk[2 * Q:, cols], mixk_raw[2 * Q:, cols], mixk[2 * Q:, cols].bitcast(f32),
                                        ALU.subtract).then_inc(mixk_set, 1)

            mixk_low(0)
            dve.wait_ge(att_hi_set, 1)
            nc.vector.tensor_copy(att_t[:, :], side[0][0:K, 0:B]).then_inc(att_t_ready, 1)
            for q in (1, 3):
                rows = slice(q * Q, (q + 1) * Q)
                nc.vector.tensor_tensor(att_parts[rows, :], side[0][rows, 0:B], att_parts[rows, :].bitcast(f32),
                                        ALU.subtract).then_inc(att_lo_set, 1)
            mixk_low(1)
            take_w(0)
            dve.wait_ge(bias_mm, 1)
            nc.vector.tensor_copy(bias_rows[:, :], side[0][:, 0:C]).then_inc(bias_ready, 1)
            take_w(1)
            for n in range(NA):
                if n % 2 == 1:
                    dve.wait_ge(agg_mm, n + 1)
                    take_agg(nc.vector.tensor_copy, n, 1, agg_dve)
                if n in W_AFTER_AGG:
                    take_w(W_AFTER_AGG[n])
            for g in W_AFTER_ALL:
                take_w(g)
            dve.wait_ge(rw_hi_set, 1)
            rw = (slice(None), slice(None), slice(D + ER, NW))
            nc.vector.tensor_tensor(w_lo[rw], side[1][:, 0:NC * E].rearrange("p (c e) -> p c e", c=NC),
                                    w_hi[rw].bitcast(f32), ALU.subtract).then_inc(rw_lo_set, 1)

            def add_bias(t, k, h):
                if h == 0:
                    dve.wait_ge(mix_w_in[k], (t - k) * (MIX_W // XR) + MIX_W)
                dve.wait_ge(mixed, 2 * t + h + 1)
                nc.vector.tensor_tensor(y_sum[:, h, :].rearrange("p (c r) -> p c r", c=HALF),
                                        y_ps[h][:, :].rearrange("p (c r) -> p c r", c=HALF),
                                        bias_sb[:, k, :].unsqueeze(1).broadcast_to([P, HALF, P]),
                                        ALU.add).then_inc(y_sum_ready, 1)

            def split_y(t, k, h):
                dve.wait_ge(y_hi_ready, 2 * t + h + 1)
                cols = slice(h * BANK, (h + 1) * BANK)
                nc.vector.tensor_tensor(y_lo[:, k % 2, cols], y_sum[:, h, :], y_hi[:, k % 2, cols].bitcast(f32),
                                        ALU.subtract).then_inc(y_lo_ready, 1)

            def route_logits(t, k):
                dve.wait_ge(main_done, t + 1)
                nc.vector.tensor_copy(logits[:, :], side[k % 2][:, SIDE + ER:SIDE + ER + E]).then_inc(route_step, 1)
                dve.wait_ge(route_step, ROUTE * t + 1)
                nc.vector.tensor_reduce(neg_max[:, :], logits[:, :], AX.X, ALU.max,
                                        negate=True).then_inc(route_step, 1)

            def route_choice(t, k):
                other = logits[:, :].unsqueeze(1).broadcast_to([P, E, E])
                own = logits[:, :].unsqueeze(2).broadcast_to([P, E, E])
                nc.vector.tensor_tensor(beats[:, :, 0:E], other, own, ALU.is_gt).then_inc(route_step, 1)
                nc.vector.tensor_tensor(ties[:, :, :], other, own, ALU.is_equal).then_inc(route_step, 1)
                dve.wait_ge(route_step, ROUTE * t + 4)
                nc.vector.tensor_tensor(beats[:, :, E:2 * E], ties[:, :, :], earlier[:, :, :],
                                        ALU.mult).then_inc(route_step, 1)
                dve.wait_ge(route_step, ROUTE * t + 5)
                nc.vector.tensor_reduce(rank[:, :], beats[:, :, :], AX.X, ALU.add).then_inc(route_step, 1)
                dve.wait_ge(route_step, ROUTE * t + 6)
                nc.vector.tensor_scalar(chosen[:, :], rank[:, :], float(TOP), None, ALU.is_lt).then_inc(route_step, 1)

            def route_weigh(t, k):
                dve.wait_ge(route_step, ROUTE * t + 7)
                dve.wait_ge(exps_ready, t + 1)
                nc.vector.tensor_tensor(picked[:, :], exps[:, :], chosen[:, :], ALU.mult).then_inc(route_step, 1)
                dve.wait_ge(route_step, ROUTE * t + 8)
                nc.vector.tensor_reduce(total[:, :], picked[:, :], AX.X, ALU.add).then_inc(route_step, 1)
                dve.wait_ge(route_step, ROUTE * t + 9)
                nc.vector.reciprocal(inv_total[:, :], total[:, :]).then_inc(route_step, 1)
                dve.wait_ge(route_step, ROUTE * t + 10)
                nc.vector.tensor_scalar(gate[:, :], picked[:, :], inv_total[:, :], SCALING,
                                        ALU.mult, ALU.mult).then_inc(route_step, 1)
                dve.wait_ge(route_step, ROUTE * t + 11)
                if from_tile(t, 1):
                    dve.wait_ge(mid_tr, t)
                nc.vector.tensor_tensor(mid[:, :].rearrange("p (e r) -> p e r", e=E),
                                        side[k % 2][:, MID].rearrange("p (e r) -> p e r", e=E),
                                        gate[:, :].unsqueeze(2).broadcast_to([P, E, R]),
                                        ALU.mult).then_inc(route_step, 1)

            def split_mid(t, k):
                dve.wait_ge(mid_hi_ready, t + 1)
                nc.vector.tensor_tensor(mid_lo[:, :], mid_ps, mid_hi[:, :].bitcast(f32),
                                        ALU.subtract).then_inc(mid_lo_ready, 1)

            def add_x(t, k, groups=(0, 1, 2)):
                if from_tile(t, 2):
                    dve.wait_ge(out_stored[k % 2], 8 * (t - k % 2))
                for n, g in enumerate(groups):
                    a, z = GROUPS[g][0], min(GROUPS[g][1], D)
                    dve.wait_ge(up_done, 3 * t + n + 1)
                    nc.vector.tensor_tensor(out_sb[:, k % 2, a:z], acc[k % 2][g][:, 0:z - a], x_sb[:, k, a:z],
                                            ALU.add).then_inc(out_ready, 1)

            add_bias(0, 0, 0)
            split_y(0, 0, 0)

            def tile(t, k):
                if from_tile(t, 1):
                    route_logits(t - 1, (k - 1) % XR)
                add_bias(t, k, 1)
                if from_tile(t, 1):
                    route_choice(t - 1, (k - 1) % XR)
                    route_weigh(t - 1, (k - 1) % XR)
                split_y(t, k, 1)
                if from_tile(t, 1):
                    split_mid(t - 1, (k - 1) % XR)
                if before_tile(t, NT - 1):
                    add_bias(t + 1, (k + 1) % XR, 0)
                    split_y(t + 1, (k + 1) % XR, 0)
                if isinstance(t, int) and t == NT - 1:
                    route_logits(t, k)
                    route_choice(t, k)
                    route_weigh(t, k)
                if from_tile(t, 1):
                    add_x(t - 1, (k - 1) % XR)

            over_tiles(dve, tile)
            last = (NT - 1, (NT - 1) % XR)
            split_mid(*last)
            add_x(*last, groups=(2, 1, 0))

    return nc


_INS = ['x', 'cond_128', 'L0_cond_W0', 'L0_cond_b0', 'L0_cond_W1', 'L0_cond_b1', 'L0_cond_W2', 'L0_cond_b2',
        'L0_cond_weight', 'L0_cond_bias_k', 'L0_ffn_base_W', 'L0_ffn_router_W', 'L0_ffn_lora_A', 'L0_ffn_lora_B']


def kernel(**inputs):
    import numpy as np
    import concourse.bacc as bacc
    from concourse.bass_utils import run_bass_kernel_spmd

    nc = bacc.Bacc("TRN2", target_bir_lowering=False, num_devices=1)
    arrays, args = {}, []
    for name in _INS:
        a = np.ascontiguousarray(inputs[name])
        arrays[f"in_{name}"] = a
        args.append(nc.dram_tensor(f"in_{name}", a.shape, mybir.dt.from_np(a.dtype), kind="ExternalInput").ap())
    shape = inputs['x'].shape
    args.append(nc.dram_tensor("out", shape, mybir.dt.float32, kind="ExternalOutput").ap())
    adaln_ffn_kernel(nc, *args)
    r = run_bass_kernel_spmd(nc, [arrays], core_ids=[0])
    return r.results[0]["out"]
```
